# Optimizing a Trainium2 kernel written in Bass

```python
import numpy as np
import jax
import jax.numpy as jnp

def _softmax(x, axis=-1):
    return jax.nn.softmax(x, axis=axis)

def _gelu(x):
    return jax.nn.gelu(x, approximate=True)

def _silu(x):
    return jax.nn.silu(x)

def _sigmoid(x):
    return jax.nn.sigmoid(x)

def _layernorm(x, axis=-1, eps=1e-05):
    m = jnp.mean(x, axis=axis, keepdims=True)
    v = jnp.var(x, axis=axis, keepdims=True)
    return (x - m) / jnp.sqrt(v + eps)

def _scatter_add(tgt, idx, src, axis=0):
    return tgt.at[idx].add(src)

def _segment_sum(src, seg, n):
    return jax.ops.segment_sum(src, seg, n)
kernel_name = 'mk_decoder_postln_d1_seqx_r8_df740a'

def setup_inputs(seed: int=0):
    np.random.seed(seed)
    _w = jnp.asarray

    def _rec_inputs():
        import jax
        import jax.numpy as jnp
        _rk = jax.random.key(seed)
        x = -7.109e-05 + 0.9999 * jax.random.normal(jax.random.fold_in(_rk, 1), (8, 56, 512), jnp.float32)
        _lenS = 56 - jax.random.randint(jax.random.fold_in(_rk, 7), (8,), 0, max(1, 56 // 4) + 1, jnp.int32)
        _lenS2 = 1500 - jax.random.randint(jax.random.fold_in(_rk, 8), (8,), 0, max(1, 1500 // 4) + 1, jnp.int32)
        _ctx_4096P = jax.random.normal(jax.random.fold_in(_rk, 11), (8, 16, 512), jnp.float32)
        _ctx_4096c = jax.random.dirichlet(jax.random.fold_in(_rk, 511), 0.3 * jnp.ones((16,), jnp.float32), (8, 1500))
        _ctx_4096t = jnp.einsum('bsk,bkd->bsd', _ctx_4096c, _ctx_4096P)
        _ctx_4096t = _ctx_4096t * jax.lax.rsqrt(jnp.mean(jnp.square(_ctx_4096t)) + 1e-12) * 0.953939
        ctx_4096 = -2.6191e-05 + 0.999952 * (_ctx_4096t + 0.3 * jax.random.normal(jax.random.fold_in(_rk, 611), (8, 1500, 512), jnp.float32))
        return (x, ctx_4096)
    x, ctx_4096 = _rec_inputs()

    def _L0_attn_setup():
        import jax, jax.numpy as jnp
        import numpy as np
        HDC_DIM = 512
        N_HEADS = 4
        HEAD_DIM = HDC_DIM // N_HEADS

        def _ste_sign(w):
            alpha = jnp.mean(jnp.abs(w), axis=-1, keepdims=True)
            hard = alpha * jnp.sign(w)
            hard = jnp.where(hard == 0, alpha, hard)
            return jax.lax.stop_gradient(hard - w) + w
        key = jax.random.key(seed)
        kx, kq, kk, kv = jax.random.split(key, 4)
        B, T = (4, 256)
        x = jax.random.normal(kx, (B, T, HDC_DIM), dtype=jnp.float32)
        bv_q = jax.random.normal(kq, (N_HEADS, HEAD_DIM), dtype=jnp.float32) * 0.02
        bv_k = jax.random.normal(kk, (N_HEADS, HEAD_DIM), dtype=jnp.float32) * 0.02
        bv_v = jax.random.normal(kv, (N_HEADS, HEAD_DIM), dtype=jnp.float32) * 0.02
        return {'x': x, 'bv_q': bv_q, 'bv_k': bv_k, 'bv_v': bv_v}
    _L0_attn_all = _L0_attn_setup()
    _L0_attn_in = {k: v for k, v in _L0_attn_all.items() if k in ('bv_q', 'bv_k', 'bv_v')}
    del _L0_attn_all

    def _L0_xattn_setup():
        import jax, jax.numpy as jnp
        import numpy as np
        TEXT_DIM = 512
        FEATURE_DIM = 512

        def _xavier_uniform(key, shape):
            fan_in, fan_out = (shape[1], shape[0])
            limit = float(np.sqrt(6.0 / (fan_in + fan_out)))
            return jax.random.uniform(key, shape, jnp.float32, -limit, limit)
        key = jax.random.key(seed)
        k1, k2, k3, k4 = jax.random.split(key, 4)
        text = jax.random.normal(k1, (8, 256, TEXT_DIM), jnp.float32)
        features = jax.random.normal(k2, (8, 72, FEATURE_DIM), jnp.float32)
        Wq = _xavier_uniform(k3, (FEATURE_DIM, TEXT_DIM))
        bq = jnp.zeros((FEATURE_DIM,), jnp.float32)
        Wk = _xavier_uniform(k4, (FEATURE_DIM, FEATURE_DIM))
        bk = jnp.zeros((FEATURE_DIM,), jnp.float32)
        return {'text': text, 'features': features, 'Wq': Wq, 'bq': bq, 'Wk': Wk, 'bk': bk}
    _L0_xattn_all = _L0_xattn_setup()
    _L0_xattn_in = {k: v for k, v in _L0_xattn_all.items() if k in ('Wq', 'bq', 'Wk', 'bk')}
    del _L0_xattn_all

    def _L0_ffn_setup():
        import jax, jax.numpy as jnp
        import numpy as np
        HIDDEN = 512
        INTER = 1376
        RANK = 128
        B, S = (2, 256)
        key = jax.random.key(seed)
        ks = jax.random.split(key, 7)
        sc = 0.02
        return {'x': jax.random.normal(ks[0], (B, S, HIDDEN), dtype=jnp.float32), 'U1': jax.random.normal(ks[1], (HIDDEN, RANK), dtype=jnp.float32) * sc, 'V1': jax.random.normal(ks[2], (RANK, 2 * INTER), dtype=jnp.float32) * sc, 'U2': jax.random.normal(ks[3], (INTER, RANK), dtype=jnp.float32) * sc, 'V2': jax.random.normal(ks[4], (RANK, HIDDEN), dtype=jnp.float32) * sc, 'b1': jax.random.normal(ks[5], (2 * INTER,), dtype=jnp.float32) * sc, 'b2': jax.random.normal(ks[6], (HIDDEN,), dtype=jnp.float32) * sc}
    _L0_ffn_all = _L0_ffn_setup()
    _L0_ffn_in = {k: v for k, v in _L0_ffn_all.items() if k in ('U1', 'V1', 'U2', 'V2', 'b1', 'b2')}
    del _L0_ffn_all
    return {'x': x, 'ctx_4096': ctx_4096, 'L0_attn_bv_q': _L0_attn_in['bv_q'], 'L0_attn_bv_k': _L0_attn_in['bv_k'], 'L0_attn_bv_v': _L0_attn_in['bv_v'], 'L0_xattn_Wq': _L0_xattn_in['Wq'], 'L0_xattn_bq': _L0_xattn_in['bq'], 'L0_xattn_Wk': _L0_xattn_in['Wk'], 'L0_xattn_bk': _L0_xattn_in['bk'], 'L0_ffn_U1': _L0_ffn_in['U1'], 'L0_ffn_V1': _L0_ffn_in['V1'], 'L0_ffn_U2': _L0_ffn_in['U2'], 'L0_ffn_V2': _L0_ffn_in['V2'], 'L0_ffn_b1': _L0_ffn_in['b1'], 'L0_ffn_b2': _L0_ffn_in['b2']}

def reference(x, ctx_4096, L0_attn_bv_q, L0_attn_bv_k, L0_attn_bv_v, L0_xattn_Wq, L0_xattn_bq, L0_xattn_Wk, L0_xattn_bk, L0_ffn_U1, L0_ffn_V1, L0_ffn_U2, L0_ffn_V2, L0_ffn_b1, L0_ffn_b2):
    import jax
    import jax.numpy as jnp

    def _L0_attn_ref(x, bv_q, bv_k, bv_v):
        import jax, jax.numpy as jnp
        import numpy as np
        HDC_DIM = 512
        N_HEADS = 4
        HEAD_DIM = HDC_DIM // N_HEADS

        def _ste_sign(w):
            alpha = jnp.mean(jnp.abs(w), axis=-1, keepdims=True)
            hard = alpha * jnp.sign(w)
            hard = jnp.where(hard == 0, alpha, hard)
            return jax.lax.stop_gradient(hard - w) + w
        B, T, D = x.shape
        H, HD = (N_HEADS, HEAD_DIM)
        scale = HD ** (-0.5)
        q_bind = _ste_sign(bv_q)
        k_bind = _ste_sign(bv_k)
        v_bind = _ste_sign(bv_v)
        xh = x.reshape(B, T, H, HD)
        Q = xh * q_bind
        K = xh * k_bind
        V = xh * v_bind
        scores = jnp.einsum('bthd,bshd->bhts', Q, K) * scale
        causal = jnp.tril(jnp.ones((T, T), dtype=bool))
        attn = jnp.where(causal, jax.nn.sigmoid(scores * 4.0), 0.0)
        out = jnp.einsum('bhts,bshd->bthd', attn, V)
        return out.reshape(B, T, D)

    def _L0_xattn_ref(text, features, Wq, bq, Wk, bk):
        import jax, jax.numpy as jnp
        import numpy as np
        TEXT_DIM = 512
        FEATURE_DIM = 512

        def _xavier_uniform(key, shape):
            fan_in, fan_out = (shape[1], shape[0])
            limit = float(np.sqrt(6.0 / (fan_in + fan_out)))
            return jax.random.uniform(key, shape, jnp.float32, -limit, limit)
        Q = jnp.einsum('btx,dx->btd', text, Wq) + bq
        K = jnp.einsum('bpx,dx->bpd', features, Wk) + bk
        scale = 1.0 / jnp.sqrt(jnp.asarray(K.shape[-1], K.dtype))
        scores = jnp.einsum('btd,bpd->btp', Q, K) * scale
        attn = jax.nn.softmax(scores, axis=-1)
        attended = jnp.einsum('btp,bpd->btd', attn, features)
        return attended

    def _L0_ffn_ref(x, U1, V1, U2, V2, b1, b2):
        import jax, jax.numpy as jnp
        import numpy as np
        HIDDEN = 512
        INTER = 1376
        RANK = 128
        B, S = (2, 256)
        P = jnp.einsum('bsh,hr->bsr', x, U1)
        H = jnp.einsum('bsr,rf->bsf', P, V1) + b1
        gate, up = (H[..., :INTER], H[..., INTER:])
        act = jax.nn.silu(gate) * up
        Z = jnp.einsum('bsi,ir->bsr', act, U2)
        out = jnp.einsum('bsr,rh->bsh', Z, V2) + b2
        return out
    x = _layernorm(x + _L0_attn_ref(x, L0_attn_bv_q, L0_attn_bv_k, L0_attn_bv_v), axis=-1)
    x = _layernorm(x + _L0_xattn_ref(x, ctx_4096, L0_xattn_Wq, L0_xattn_bq, L0_xattn_Wk, L0_xattn_bk), axis=-1)
    x = _layernorm(x + _L0_ffn_ref(x, L0_ffn_U1, L0_ffn_V1, L0_ffn_U2, L0_ffn_V2, L0_ffn_b1, L0_ffn_b2), axis=-1)
    return x

_drawn_inputs = setup_inputs


def setup_inputs(seed=0):
    import zlib

    import numpy as np

    out = dict(_drawn_inputs(seed))
    spreads = {'L0_xattn_bq': (0.0, 0.454), 'L0_xattn_bk': (0.0, 2.0)}
    factors = {'L0_attn_bv_q': 64.0,
     'L0_attn_bv_k': 64.0,
     'L0_ffn_U1': 8.0,
     'L0_ffn_V1': 8.0,
     'L0_ffn_U2': 8.0,
     'L0_ffn_V2': 8.0,
     'L0_ffn_b1': 8.0,
     'L0_ffn_b2': 22.056}
    for name, (base, spread) in spreads.items():
        noise = np.random.default_rng([zlib.crc32(name.encode()), seed]).standard_normal(out[name].shape)
        drawn = base * np.exp(spread * noise) if base else spread * noise
        out[name] = jnp.asarray(drawn.astype(out[name].dtype))
    for name, factor in factors.items():
        out[name] = (out[name] * factor).astype(out[name].dtype)
    return out
```

```python
from contextlib import ExitStack

import concourse.bass as bass
from concourse import mybir

F32 = mybir.dt.float32
ALU = mybir.AluOpType
ACT = mybir.ActivationFunctionType
AX = mybir.AxisListType

P = 128
EPS = 1e-5



def steps(pairs, groups, chunks):
    out = []
    for i in range(pairs + 2):
        if i < pairs:
            out.append(("xT", i))
        if 1 <= i <= pairs:
            out.append(("self_scores", i - 1))
        if i >= 2:
            out.append(("self_out", i - 2))
            out.append(("wqT", i - 2))
    out += [("norm1", 0), ("ctxT", 0, 0), ("norm1", 1), ("x1T", 0), ("x1T", 1),
            ("norm1", 2), ("norm1", 3), ("ctxT", 0, 1), ("x1T", 2), ("x1T", 3)]
    out += [("q", m) for m in range(4)]
    out += [("c", p) for p in range(pairs)]
    out += [("g", m) for m in range(4)]
    last = groups - 1
    for j in range(pairs):
        for g in range(groups):
            out.append(("scores", j, g))
            if g == 0:
                out.append(("ctxT", j, last))
                if j > 0:
                    out += [("norm2", j - 1)]
        out.append(("softmax", j))
        if j > 0:
            out.append(("x2T", j - 1))
        if j + 1 < pairs:
            out += [("ctxT", j + 1, g) for g in range(groups - 1)]
        else:
            out += [("proj", (0, 1))] + [("ffn", (0, 1), c) for c in range(chunks)] + [("ffn_out", (0, 1))]
        out += [("pT", j), ("attend", j)]
    out += [("proj", (2,))] + [("ffn", (2,), c) for c in range(chunks)]
    out += [("ffn_out", (2,)), ("norm2", 3), ("x2T", 3)]
    out += [("proj", (3,))] + [("ffn", (3,), c) for c in range(chunks)] + [("ffn_out", (3,))]
    return out


def decoder_layer(nc, x, ctx, bv_q, bv_k, bv_v, Wq, bq, Wk, bk, U1, V1, U2, V2, b1, b2, out):
    B, T, D = x.shape
    S = ctx.shape[1]
    H, HD = bv_q.shape
    R = U1.shape[1]
    INTER = U2.shape[0]
    PAIRS = B // 2
    TP = P // 2
    KD = D // P
    KT = 12
    Q = S // KT
    GROUPS = 3
    KG = KT // GROUPS
    GC = KG * Q
    FC = -(-INTER // P)
    FT = INTER - (FC - 1) * P
    SLOTS = 4
    SELF_SCALE = 4.0 * float(HD) ** -0.5
    X_SCALE = float(D) ** -0.5
    QA = 112
    assert D == 512 and HD == P and H == KD and R == P and Q * KT == S and Q <= P and GC <= 512
    assert PAIRS == 4 and T <= TP

    STEPS = steps(PAIRS, GROUPS, FC)

    es = ExitStack()
    with es:
        def sb(name, shape):
            return es.enter_context(nc.sbuf_tensor(name, shape, F32))

        def ps(name, shape):
            return es.enter_context(nc.psum_tensor(name, shape, F32))

        def sem(name):
            return es.enter_context(nc.semaphore(name))

        ctx_sb = sb("ctx_sb", [P, SLOTS, KT, D])
        ctxT = sb("ctxT", [P, 2, 2, KD, GC])
        prob = sb("prob", [P, KT, Q])
        probT = sb("probT", [P, KT, P])
        X = sb("X", [P, PAIRS, D])
        gT = sb("gT", [P, KD, B, TP])
        u2 = sb("u2", [P, FC, R])
        b2_rows = sb("b2_rows", [P, D])
        shared = sb("shared", [P, 8192 + KD * B * T])
        wkv = shared[:, 0:2048].rearrange("p (k x) -> p k x", k=KD)
        wqT = shared[:, 2048:4096].rearrange("p (k x) -> p k x", k=KD)
        qT = shared[:, 4096:6144].rearrange("p (k b t) -> p k b t", k=KD, b=B)
        x1T = shared[:, 6144:6144 + KD * B * T].rearrange("p (k b t) -> p k b t", k=KD, b=B)
        NMAX = 4 * T
        v1 = shared[:, 0:2 * INTER]
        at = 2 * INTER
        x2T = shared[:, at:at + KD * B * T].rearrange("p (k n) -> p k n", k=KD)
        at += KD * B * T
        prT = shared[:, at:at + NMAX]
        at += NMAX
        act = shared[:, at:at + FC * NMAX].rearrange("p (c n) -> p c n", c=FC)
        at += FC * NMAX
        gate = shared[:, at:at + 2 * NMAX].rearrange("p (a n) -> p a n", a=2)
        at += 2 * NMAX
        tanh = shared[:, at:at + 2 * NMAX].rearrange("p (a n) -> p a n", a=2)
        at += 2 * NMAX
        u1 = shared[:, at:at + KD * R].rearrange("p (k r) -> p k r", k=KD)
        at += KD * R
        v2 = shared[:, at:at + D]
        at += D
        assert at <= 8192 + KD * B * T
        zT = sb("zT", [P, 2, 2, TP])
        early = ctx_sb[:, SLOTS - 1].rearrange("p k x -> p (k x)")
        wq = early[:, 0:2048].rearrange("p (k x) -> p k x", k=KD)
        xT = early[:, 2048:3072].rearrange("p (a h t) -> p a h t", a=2, h=H)
        kqT = early[:, 3072:4096].rearrange("p (a h t) -> p a h t", a=2, h=H)
        selfp = early[:, 4096:5120].rearrange("p (a h t) -> p a h t", a=2, h=H)
        val = early[:, 5120:6144].rearrange("p (a n) -> p a n", a=2)

        ident = sb("ident", [P, P])
        mask = sb("mask", [P, P])
        NROW = 2 * KD + 2 * FC
        start = prob[:, :, :].rearrange("p k q -> p (k q)")
        vdiag = start[0:H, 0:D].rearrange("p (h d) -> p h d", h=H)
        sign = start[0:H, D:D + 3 * P].rearrange("p (a d) -> p a d", a=3)
        ones = start[0:H, D + 3 * P:D + 4 * P]
        rows = start[0:NROW, D + 4 * P:D + 5 * P]
        bv = probT[0:H, H:H + 3, :]
        bound = probT[0:H, H + 4:H + 7, :]
        qk = probT[0:H, H + 3, :]
        v_rows = probT[:, 0:H, :].rearrange("p h d -> p (h d)")
        cols = sb("cols", [P, 2 * KD + 2 * FC])
        hcols = sb("hcols", [P, 2 * FC])
        alpha = sb("alpha", [H, 3])
        qkc = sb("qkc", [P, H])
        c_sb = sb("c_sb", [P, PAIRS])
        top = sb("top", [P, GROUPS])
        topc = sb("topc", [P, 1])
        bias = sb("bias", [P, 1])
        den = sb("den", [P, GROUPS])
        dsum = sb("dsum", [P, 1])
        rden = sb("rden", [P, 1])
        stats = sb("stats", [P, 3, PAIRS, 6])
        mv = sb("mv", [P, 3, PAIRS, 2])
        veps = sb("veps", [P, 3, PAIRS])
        rstd = sb("rstd", [P, 3, PAIRS])
        mhalf = sb("mhalf", [P, 1])

        psS = ps("psS", [P, GROUPS, 512])
        psT = ps("psT", [P, 2, 512])
        psW = ps("psW", [P, 2, 512])
        psA = ps("psA", [P, 512])

        x_in = [sem(f"x_in{p}") for p in range(PAIRS)]
        bv_in, rows_in, b2_in = sem("bv_in"), sem("rows_in"), sem("b2_in")
        wq_in, wk_in, v1_in, u_in = sem("wq_in"), sem("wk_in"), sem("v1_in"), sem("u_in")
        ctx_in = [[sem(f"ctx_in{s}_{g}") for g in range(GROUPS)] for s in range(SLOTS)]
        rows_zero = sem("rows_zero")
        consts = sem("consts")
        pool_chain = sem("pool_chain")
        dve_chain = sem("dve_chain")
        qkv_ready = sem("qkv_ready")
        vdiag_ready = sem("vdiag_ready")
        cols_ready = sem("cols_ready")
        v_rows_ready = sem("v_rows_ready")
        kq_ready = sem("kq_ready")
        val_ready = sem("val_ready")
        tanh_ready = sem("tanh_ready")
        selfp_ready = sem("selfp_ready")
        var_ready = sem("var_ready")
        rstd_ready = sem("rstd_ready")
        x1_ready = sem("x1_ready")
        x2_ready = sem("x2_ready")
        x2b_ready = sem("x2b_ready")
        q_ready, c_ready, g_ready = sem("q_ready"), sem("c_ready"), sem("g_ready")
        scored = sem("scored")
        bias_ready = sem("bias_ready")
        exp_ready = sem("exp_ready")
        attended = sem("attended")
        turn_full = [sem("turn_full_act"), sem("turn_full_dve")]
        turned = [sem("turned_act"), sem("turned_dve")]
        work_full = [sem("work_full0"), sem("work_full1")]
        v_bound = sem("v_bound")
        summed = sem("summed")
        self_added = sem("self_added")
        att_added = sem("att_added")
        y_added = sem("y_added")
        pr_ready = sem("pr_ready")
        gate_ready = sem("gate_ready")
        act_ready = sem("act_ready")
        z_ready = sem("z_ready")
        y_ready = sem("y_ready")
        out_sem = sem("out_sem")

        FFN_COUNT = {g: i for i, g in enumerate(((0, 1), (2,), (3,)))}
        turn_of, work_of = {}, {}
        n_turn = n_work = 0
        work_of["setup"], n_work = 0, 1
        work_read = [(cols_ready, 1)]
        acc_read = [(v_rows_ready, 1)]
        for s in STEPS:
            kind = s[0]
            k = {"xT": 1, "wqT": 1, "x1T": 1, "x2T": 1, "ctxT": 2 * KD, "pT": GROUPS}.get(kind, 0)
            if k:
                turn_of[s] = n_turn
                n_turn += k
            read = {"self_scores": tanh_ready, "self_out": self_added, "q": q_ready, "c": c_ready,
                    "g": g_ready, "proj": pr_ready, "ffn": act_ready, "ffn_out": y_added}.get(kind)
            if read is not None:
                work_of[s] = n_work
                if kind == "proj":
                    done = [FFN_COUNT[s[1]] + 1]
                elif kind == "ffn":
                    done = [FFN_COUNT[s[1]] * FC + s[2] + 1]
                elif kind == "ffn_out":
                    done = [p + 1 for p in s[1]]
                else:
                    done = [s[1] + 1]
                work_read += [(read, d) for d in done]
                n_work += len(done)
            if kind == "attend":
                acc_read.append((att_added, s[1] + 1))
            if kind == "ffn_out":
                acc_read.append((z_ready, FFN_COUNT[s[1]] + 1))

        def wait_turned(eng, first, count=1):
            for bank in range(2):
                last = max((n for n in range(first, first + count) if n % 2 == bank), default=None)
                if last is not None:
                    eng.wait_ge(turned[bank], last // 2 + 1)

        def turned_into(step, i):
            n = turn_of[step] + i
            bank = psT[:, n % 2]
            kind = step[0]
            if kind == "xT":
                return xT[:, step[1] % 2], bank.rearrange("p (h t) -> p h t", h=H)
            if kind == "wqT":
                m = step[1]
                return wqT[:, :, m * P:(m + 1) * P], bank.rearrange("p (k t) -> p k t", k=KD)
            if kind in ("x1T", "x2T"):
                src = bank.rearrange("p (k b t) -> p k b t", k=KD, b=2)[:, :, :, 0:T]
                p = step[1]
                if kind == "x1T":
                    return x1T[:, :, 2 * p:2 * p + 2, :], src
                return x2T[:, :, 2 * T * p:2 * T * (p + 1)].rearrange("p k (b t) -> p k b t", b=2), src
            if kind == "ctxT":
                _, j, g = step
                return ctxT[:, (GROUPS * j + g) % 2, i // KD, i % KD, :], bank[:, 0:GC]
            return probT[0:Q, KG * i:KG * i + KG, :], bank[0:Q].rearrange("p (k t) -> p k t", k=KG)

        def columns(group):
            return len(group) * 2 * T

        def piece(c):
            return P if c < FC - 1 else FT

        block = es.enter_context(nc.Block())

        @block.sync
        def _(sp):
            for p in range(PAIRS):
                src = x[2 * p:2 * p + 2].rearrange("b t x -> (b t) x")
                for h in range(2):
                    r0 = (2 * p + h) * T
                    n = min(TP, B * T - r0)
                    flat = x.rearrange("b t x -> (b t) x")
                    sp.dma_start(X[h * TP:h * TP + n, p, :], flat[r0:r0 + n, :]).then_inc(x_in[p], 16)
                    if n < TP:
                        sp.dma_start(X[h * TP + n:(h + 1) * TP, p, :], flat[0:TP - n, :]).then_inc(x_in[p], 16)
            sp.dma_start(wq, Wq.rearrange("(k p) x -> p k x", p=P)).then_inc(wq_in, 16)

            def load_ctx(b, g):
                slot = b % SLOTS
                if b >= SLOTS:
                    sp.wait_ge(attended, GROUPS * (b // 2 - SLOTS // 2) + g + 1)
                v = ctx[b].rearrange("(q k) x -> q k x", k=KT)
                ks = slice(KG * g, KG * g + KG)
                for q0, q1 in ((0, QA), (QA, Q)):
                    sp.dma_start(ctx_sb[q0:q1, slot, ks, :], v[q0:q1, ks, :]).then_inc(ctx_in[slot][g], 16)

            for g in range(GROUPS):
                for b in range(2):
                    load_ctx(b, g)
                if g == 0:
                    sp.dma_start(wkv, Wk.rearrange("(k p) x -> p k x", p=P)).then_inc(wk_in, 16)
            n = work_of[("self_out", PAIRS - 1)]
            for g in range(GROUPS):
                load_ctx(2, g)
                if g == 0:
                    sp.wait_ge(work_full[n % 2], n // 2 + 1)
                    n = turn_of[("wqT", KD - 1)]
                    sp.wait_ge(turn_full[n % 2], n // 2 + 1)
                load_ctx(3, g)
            sp.dma_start(u2[:, 0:FC - 1, :], U2[0:(FC - 1) * P].rearrange("(c p) r -> p c r", p=P)).then_inc(u_in, 16)
            sp.dma_start(u2[0:FT, FC - 1, :], U2[(FC - 1) * P:INTER]).then_inc(u_in, 16)
            n = work_of[("g", KD - 1)]
            sp.wait_ge(work_full[n % 2], n // 2 + 1)
            sp.dma_start(v1, V1).then_inc(v1_in, 16)
            sp.dma_start(u1, U1.rearrange("(k p) r -> p k r", p=P)).then_inc(u_in, 16)
            sp.dma_start(v2, V2).then_inc(u_in, 16)
            for j in range(SLOTS // 2, PAIRS):
                for g in range(GROUPS):
                    load_ctx(2 * j, g)
                    load_ctx(2 * j + 1, g)
            for p in range(PAIRS):
                sp.wait_ge(y_ready, p + 1)
                for h in range(2):
                    sp.dma_start(out[2 * p + h], X[h * TP:h * TP + T, p, :]).then_inc(out_sem, 16)
            sp.wait_ge(out_sem, 16 * B)

        @block.gpsimd
        def _(pool):
            chained = [0]

            def link(ins):
                chained[0] += 1
                ins.then_inc(pool_chain, 1)
                pool.wait_ge(pool_chain, chained[0])

            link(nc.gpsimd.memset(ident[:, :], 0.0))
            nc.gpsimd.affine_select(out=ident[:, :], in_=ident[:, :], compare_op=ALU.not_equal, fill=1.0,
                                    base=0, pattern=[[-1, P]], channel_multiplier=1).then_inc(consts, 1)
            nc.gpsimd.memset(ones[:, :], 1.0)
            nc.gpsimd.memset(mhalf[:, :], -0.5)
            link(nc.gpsimd.memset(mask[:, :], 0.5))
            link(nc.gpsimd.affine_select(out=mask[:, :], in_=mask[:, :], compare_op=ALU.is_ge, fill=0.0,
                                         base=0, pattern=[[1, P]], channel_multiplier=-1))
            nc.gpsimd.memset(mask[0:TP, TP:P], 0.0).then_inc(consts, 1)
            pool.wait_ge(qkv_ready, 1)
            nc.gpsimd.affine_select(out=vdiag[:, :, :], in_=bv[:, 2:3, :].to_broadcast([H, H, P]),
                                    compare_op=ALU.is_equal, fill=0.0, base=0,
                                    pattern=[[-1, H], [0, P]], channel_multiplier=1).then_inc(vdiag_ready, 1)
            nc.gpsimd.memset(qT[:, :, :, T:TP], 0.0)
            nc.gpsimd.memset(gT[:, :, :, T:TP], 0.0)
            nc.gpsimd.memset(zT[:, :, :, T:TP], 0.0).then_inc(consts, 1)
            pool.wait_ge(v_rows_ready, 1)
            norms = 0

            def inverse_deviation(layer, p):
                nonlocal norms
                norms += 1
                pool.wait_ge(var_ready, norms)
                link(nc.gpsimd.tensor_scalar(veps[:, layer, p:p + 1], mv[:, layer, p, 1:2], EPS, None, ALU.add))
                nc.gpsimd.tensor_tensor(rstd[:, layer, p:p + 1], veps[:, layer, p:p + 1], mhalf[:, :],
                                        ALU.pow).then_inc(rstd_ready, 1)

            for step in STEPS:
                kind = step[0]
                if kind == "xT":
                    p = step[1]
                    pool.wait_ge(x_in[p], 16 * (2 if p < PAIRS - 1 else 3))
                    if p >= 2:
                        n = work_of[("self_out", p - 2)]
                        pool.wait_ge(work_full[n % 2], n // 2 + 1)
                    nc.gpsimd.tensor_tensor(val[:, p % 2, :], X[:, p, :], v_rows[:, :],
                                            ALU.mult).then_inc(val_ready, 1)
                elif kind == "self_out":
                    inverse_deviation(0, step[1])
                elif kind == "attend":
                    inverse_deviation(1, step[1])
                elif kind == "ffn_out":
                    for p in step[1]:
                        inverse_deviation(2, p)
                elif kind == "x2T":
                    p = step[1]
                    n = turn_of[step]
                    pool.wait_ge(b2_in, 16)
                    pool.wait_ge(turn_full[n % 2], n // 2 + 1)
                    nc.gpsimd.tensor_tensor(X[:, p, :], X[:, p, :], b2_rows[:, :], ALU.add).then_inc(x2b_ready, 1)

        @block.scalar
        def _(sc):
            for i, src in enumerate((bv_q, bv_k, bv_v)):
                sc.dma_start(bv[:, i, :], src).then_inc(bv_in, 16)
            sc.wait_ge(rows_zero, 1)
            r = 0
            sc.dma_start(rows[0:KD, :], bq.rearrange("(k p) -> k p", p=P)).then_inc(rows_in, 16)
            sc.dma_start(rows[KD:2 * KD, :], bk.rearrange("(k p) -> k p", p=P)).then_inc(rows_in, 16)
            for h in range(2):
                r, o = 2 * KD + h * FC, h * INTER
                sc.dma_start(rows[r:r + FC - 1, :], b1[o:o + (FC - 1) * P].rearrange("(k p) -> k p", p=P))\
                  .then_inc(rows_in, 16)
                sc.dma_start(rows[r + FC - 1:r + FC, 0:FT],
                             b1[o + (FC - 1) * P:o + INTER].rearrange("(a p) -> a p", a=1)).then_inc(rows_in, 16)
            sc.dma_start(b2_rows[:, :], b2.rearrange("(a n) -> a n", a=1).to_broadcast([P, D])).then_inc(b2_in, 16)

            sc.wait_ge(v_bound, 1)
            nc.scalar.activation(v_rows[:, :], psA[:, :], ACT.Copy).then_inc(v_rows_ready, 1)

            def empty_turns(step, count):
                for i in range(count):
                    n = turn_of[step] + i
                    if n % 2 == 0:
                        sc.wait_ge(turn_full[0], n // 2 + 1)
                        o, src = turned_into(step, i)
                        nc.scalar.activation(o, src, ACT.Copy).then_inc(turned[0], 1)

            for step in STEPS:
                kind = step[0]
                if kind == "xT":
                    p = step[1]
                    if p >= 2 and turn_of[step] % 2 == 0:
                        n = work_of[("self_scores", p - 2)]
                        sc.wait_ge(work_full[n % 2], n // 2 + 1)
                    empty_turns(step, 1)
                elif kind in ("wqT", "x1T"):
                    empty_turns(step, 1)
                elif kind == "x2T":
                    if step[1] == 0:
                        sc.wait_ge(v1_in, 16)
                    empty_turns(step, 1)
                elif kind == "ctxT":
                    _, j, g = step
                    n = GROUPS * j + g
                    if n >= 2:
                        sc.wait_ge(scored, n - 1)
                    empty_turns(step, 2 * KD)
                elif kind == "pT":
                    if step[1] >= 1:
                        sc.wait_ge(attended, GROUPS * step[1])
                    empty_turns(step, GROUPS)
                elif kind == "self_scores":
                    p, n = step[1], work_of[step]
                    sc.wait_ge(work_full[n % 2], n // 2 + 1)
                    if p >= 2:
                        m = work_of[("self_out", p - 2)]
                        sc.wait_ge(work_full[m % 2], m // 2 + 1)
                    nc.scalar.activation(selfp[:, p % 2], psW[:, n % 2].rearrange("p (h t) -> p h t", h=H),
                                         ACT.Tanh, scale=0.5 * SELF_SCALE).then_inc(tanh_ready, 1)
                elif kind == "q":
                    m, n = step[1], work_of[step]
                    sc.wait_ge(work_full[n % 2], n // 2 + 1)
                    if m == 0:
                        sc.wait_ge(consts, 3)
                        sc.wait_ge(cols_ready, 1)
                    nc.scalar.activation(qT[:, m, :, 0:T],
                                         psW[:, n % 2, 0:B * T].rearrange("p (b t) -> p b t", b=B),
                                         ACT.Identity, bias=cols[:, m:m + 1]).then_inc(q_ready, 1)
                elif kind == "g":
                    m, n = step[1], work_of[step]
                    sc.wait_ge(work_full[n % 2], n // 2 + 1)
                    nc.scalar.activation(gT[:, m, :, 0:T],
                                         psW[:, n % 2, 0:B * T].rearrange("p (b t) -> p b t", b=B),
                                         ACT.Copy).then_inc(g_ready, 1)
                elif kind == "softmax":
                    j = step[1]
                    sc.wait_ge(bias_ready, j + 1)
                    if j >= 1:
                        n = turn_of[("pT", j - 1)] + GROUPS - 1
                        sc.wait_ge(turn_full[n % 2], n // 2 + 1)
                    for g in range(GROUPS):
                        nc.scalar.activation(prob[:, KG * g:KG * g + KG, :],
                                             psS[:, g, 0:GC].rearrange("p (k q) -> p k q", k=KG),
                                             ACT.Exp, bias=bias[:, :], scale=X_SCALE,
                                             accum_out=den[:, g:g + 1]).then_inc(exp_ready, 1)
                elif kind == "proj":
                    n, N = work_of[step], columns(step[1])
                    sc.wait_ge(work_full[n % 2], n // 2 + 1)
                    nc.scalar.activation(prT[:, 0:N], psW[:, n % 2, 0:N], ACT.Copy).then_inc(pr_ready, 1)
                elif kind == "ffn":
                    _, group, c = step
                    n, N, f = work_of[step], columns(group), piece(step[2])
                    i = FFN_COUNT[group] * FC + c
                    sc.wait_ge(work_full[n % 2], n // 2 + 1)
                    if i >= 2:
                        sc.wait_ge(act_ready, i - 1)
                    nc.scalar.activation(tanh[0:f, i % 2, 0:N], psW[0:f, n % 2, 0:N], ACT.Tanh,
                                         bias=hcols[0:f, c:c + 1], scale=0.5)
                    nc.scalar.activation(gate[0:f, i % 2, 0:N], psW[0:f, n % 2, 0:N], ACT.Identity,
                                         bias=cols[0:f, 2 * KD + c:2 * KD + c + 1]).then_inc(gate_ready, 1)
                elif kind == "ffn_out":
                    group = step[1]
                    sc.wait_ge(summed, FFN_COUNT[group] + 1)
                    nc.scalar.activation(zT[:, 0:len(group), :, 0:T],
                                         psA[:, 0:columns(group)].rearrange("p (a b t) -> p a b t", b=2, t=T),
                                         ACT.Copy, scale=0.5).then_inc(z_ready, 1)

        @block.tensor
        def _(pe):
            def next_turn(n):
                if n >= 2:
                    pe.wait_ge(turned[n % 2], n // 2)
                return psT[:, n % 2]

            def next_work(n):
                if n >= 2:
                    pe.wait_ge(*work_read[n - 2])
                return psW[:, n % 2]

            acc_jobs = [1]

            def next_acc():
                pe.wait_ge(*acc_read[acc_jobs[0] - 1])
                acc_jobs[0] += 1

            pe.wait_ge(consts, 1)
            pe.wait_ge(rows_in, 16 * 6)
            nrow = 2 * KD + 2 * FC
            pe.transpose(psW[:, 0, 0:nrow], rows[:, :], ident[0:nrow, 0:nrow])
            pe.wait_ge(qkv_ready, 1)
            pe.transpose(psW[:, 0, 64:64 + H], qk, ident[0:H, 0:H]).then_inc(work_full[0], 1)
            pe.wait_ge(vdiag_ready, 1)
            pe.matmul(psA[:, :], ones[:, :], vdiag[:, :, :].rearrange("k h d -> k (h d)"),
                      start=True, stop=True).then_inc(v_bound, 1)

            def inner_sum(group, c):
                i, N, f = FFN_COUNT[group] * FC + c, columns(group), piece(c)
                pe.wait_ge(act_ready, i + 1)
                mm = pe.matmul(psA[:, 0:N], u2[0:f, c, :], act[0:f, c, 0:N], start=(c == 0), stop=(c == FC - 1))
                if c == FC - 1:
                    mm.then_inc(summed, 1)

            for step in STEPS:
                kind = step[0]
                if kind == "xT":
                    p, n = step[1], turn_of[step]
                    pe.wait_ge(x_in[p], 16 * (2 if p < PAIRS - 1 else 3))
                    bank = next_turn(n)
                    for h in range(H):
                        mm = pe.transpose(bank[:, h * P:(h + 1) * P], X[:, p, h * P:(h + 1) * P], ident[:, :])
                    mm.then_inc(turn_full[n % 2], 1)
                elif kind == "self_scores":
                    p, n = step[1], work_of[step]
                    bank = next_work(n)
                    pe.wait_ge(kq_ready, p + 1)
                    for h in range(H):
                        mm = pe.matmul(bank[:, h * P:(h + 1) * P], kqT[:, p % 2, h, :], xT[:, p % 2, h, :],
                                       start=True, stop=True)
                    mm.then_inc(work_full[n % 2], 1)
                elif kind == "self_out":
                    p, n = step[1], work_of[step]
                    bank = next_work(n)
                    pe.wait_ge(selfp_ready, p + 1)
                    pe.wait_ge(val_ready, p + 1)
                    for h in range(H):
                        mm = pe.matmul(bank[:, h * P:(h + 1) * P], selfp[:, p % 2, h, :],
                                       val[:, p % 2, h * P:(h + 1) * P], start=True, stop=True)
                    mm.then_inc(work_full[n % 2], 1)
                elif kind == "wqT":
                    m, n = step[1], turn_of[step]
                    if m == 0:
                        pe.wait_ge(wq_in, 16)
                    bank = next_turn(n)
                    for k in range(KD):
                        mm = pe.transpose(bank[:, k * P:(k + 1) * P], wq[:, m, k * P:(k + 1) * P], ident[:, :])
                    mm.then_inc(turn_full[n % 2], 1)
                elif kind in ("x1T", "x2T"):
                    p, n = step[1], turn_of[step]
                    pe.wait_ge(x1_ready if kind == "x1T" else x2_ready, p + 1)
                    bank = next_turn(n)
                    for k in range(KD):
                        mm = pe.transpose(bank[:, k * P:(k + 1) * P], X[:, p, k * P:(k + 1) * P], ident[:, :])
                    mm.then_inc(turn_full[n % 2], 1)
                elif kind == "q":
                    m, n = step[1], work_of[step]
                    if m == 0:
                        wait_turned(pe, turn_of[("x1T", PAIRS - 2)], 1)
                        wait_turned(pe, turn_of[("x1T", PAIRS - 1)], 1)
                    bank = next_work(n)
                    for k in range(KD):
                        mm = pe.matmul(bank[:, 0:B * T], wqT[:, k, m * P:(m + 1) * P],
                                       x1T[:, k, :, :].rearrange("p b t -> p (b t)"), start=(k == 0), stop=(k == KD - 1))
                    mm.then_inc(work_full[n % 2], 1)
                elif kind == "c":
                    p, n = step[1], work_of[step]
                    pe.wait_ge(q_ready, KD)
                    bank = next_work(n)
                    for k in range(KD):
                        mm = pe.matmul(bank[:, 0:1], qT[:, k, 2 * p:2 * p + 2, :].rearrange("p b t -> p (b t)"),
                                       cols[:, KD + k:KD + k + 1], start=(k == 0), stop=(k == KD - 1))
                    mm.then_inc(work_full[n % 2], 1)
                elif kind == "g":
                    m, n = step[1], work_of[step]
                    if m == 0:
                        pe.wait_ge(wk_in, 16)
                    bank = next_work(n)
                    for k in range(KD):
                        mm = pe.matmul(bank[:, 0:B * T], wkv[:, k, m * P:(m + 1) * P], qT[:, k, :, 0:T],
                                       start=(k == 0), stop=(k == KD - 1))
                    mm.then_inc(work_full[n % 2], 1)
                elif kind == "ctxT":
                    _, j, g = step
                    for h in range(2):
                        b = 2 * j + h
                        pe.wait_ge(ctx_in[b % SLOTS][g], 32 * (b // SLOTS + 1))
                        for kd in range(KD):
                            n = turn_of[step] + h * KD + kd
                            bank = next_turn(n)
                            for k in range(KG):
                                mm = pe.transpose(bank[:, k * Q:(k + 1) * Q],
                                                  ctx_sb[0:Q, b % SLOTS, KG * g + k, kd * P:(kd + 1) * P],
                                                  ident[0:Q, 0:Q])
                            mm.then_inc(turn_full[n % 2], 1)
                elif kind == "scores":
                    _, j, g = step
                    if j == 0 and g == 0:
                        pe.wait_ge(g_ready, KD)
                    if j >= 1:
                        pe.wait_ge(exp_ready, GROUPS * (j - 1) + g + 1)
                    wait_turned(pe, turn_of[("ctxT", j, g)], 2 * KD)
                    for kd in range(KD):
                        for h in range(2):
                            mm = pe.matmul(psS[h * TP:(h + 1) * TP, g, 0:GC], gT[:, kd, 2 * j + h, :],
                                           ctxT[:, (GROUPS * j + g) % 2, h, kd, :],
                                           start=(kd == 0), stop=(kd == KD - 1))
                    mm.then_inc(scored, 1)
                elif kind == "pT":
                    j = step[1]
                    for g in range(GROUPS):
                        n = turn_of[step] + g
                        pe.wait_ge(exp_ready, GROUPS * j + g + 1)
                        bank = next_turn(n)
                        for k in range(KG):
                            mm = pe.transpose(bank[0:Q, k * P:(k + 1) * P], prob[:, KG * g + k, :], ident[:, :])
                        mm.then_inc(turn_full[n % 2], 1)
                elif kind == "attend":
                    j = step[1]
                    next_acc()
                    for g in range(GROUPS):
                        wait_turned(pe, turn_of[("pT", j)] + g)
                        for k in range(KG * g, KG * g + KG):
                            for h in range(2):
                                mm = pe.matmul(psA[h * TP:(h + 1) * TP, :], probT[0:Q, k, h * TP:(h + 1) * TP],
                                               ctx_sb[0:Q, (2 * j + h) % SLOTS, k, :],
                                               start=(k == 0), stop=(k == KT - 1))
                        mm.then_inc(attended, 1)
                elif kind == "proj":
                    group = step[1]
                    n, N = work_of[step], columns(group)
                    if group[0] == 0:
                        pe.wait_ge(u_in, 16 * 4)
                        pe.wait_ge(v1_in, 16)
                    for p in group:
                        wait_turned(pe, turn_of[("x2T", p)])
                    bank = next_work(n)
                    for k in range(KD):
                        mm = pe.matmul(bank[:, 0:N], u1[:, k, :], x2T[:, k, 2 * T * group[0]:2 * T * group[0] + N], start=(k == 0), stop=(k == KD - 1))
                    mm.then_inc(work_full[n % 2], 1)
                elif kind == "ffn":
                    _, group, c = step
                    n, N, f = work_of[step], columns(group), piece(c)
                    if c == 0:
                        pe.wait_ge(pr_ready, FFN_COUNT[group] + 1)
                        next_acc()
                    bank = next_work(n)
                    pe.matmul(bank[0:f, 0:N], v1[:, c * P:c * P + f], prT[:, 0:N], start=True, stop=True)
                    pe.matmul(bank[0:f, 256:256 + N], v1[:, INTER + c * P:INTER + c * P + f], prT[:, 0:N],
                              start=True, stop=True).then_inc(work_full[n % 2], 1)
                    if c >= 2:
                        inner_sum(group, c - 2)
                elif kind == "ffn_out":
                    group = step[1]
                    inner_sum(group, FC - 2)
                    inner_sum(group, FC - 1)
                    pe.wait_ge(z_ready, FFN_COUNT[group] + 1)
                    for i in range(len(group)):
                        n = work_of[step] + i
                        bank = next_work(n)
                        pe.matmul(bank[:, :], zT[:, i].rearrange("p b t -> p (b t)"), v2[:, :],
                                  start=True, stop=True).then_inc(work_full[n % 2], 1)

        @block.vector
        def _(ve):
            chained = [0]

            def link(ins):
                chained[0] += 1
                ins.then_inc(dve_chain, 1)
                ve.wait_ge(dve_chain, chained[0])

            nc.vector.memset(rows[:, :], 0.0).then_inc(rows_zero, 1)
            ve.wait_ge(bv_in, 48)
            link(nc.vector.tensor_scalar(sign[:, :, :], bv[:, :, :], 0.0, 2.0, ALU.is_ge, ALU.mult))
            link(nc.vector.tensor_scalar(sign[:, :, :], sign[:, :, :], -1.0, None, ALU.add))
            link(nc.vector.tensor_tensor(bound[:, :, :], bv[:, :, :], sign[:, :, :], ALU.mult))
            link(nc.vector.reduce_sum(alpha[:, :], bound[:, :, :], AX.X))
            link(nc.vector.tensor_scalar(alpha[:, :], alpha[:, :], 1.0 / HD, None, ALU.mult))
            for i in range(3):
                last = nc.vector.tensor_scalar(bound[:, i, :], sign[:, i, :], alpha[:, i:i + 1], None, ALU.mult)
            link(last)
            link(nc.vector.tensor_tensor(bound[:, :, :], bound[:, :, :], bv[:, :, :], ALU.subtract))
            link(nc.vector.tensor_tensor(bv[:, :, :], bound[:, :, :], bv[:, :, :], ALU.add))
            nc.vector.tensor_tensor(qk, bv[:, 0, :], bv[:, 1, :], ALU.mult).then_inc(qkv_ready, 1)
            ve.wait_ge(work_full[0], 1)
            nrow = 2 * KD + 2 * FC
            nc.vector.tensor_copy(qkc[:, :], psW[:, 0, 64:64 + H])
            link(nc.vector.tensor_copy(cols[:, :], psW[:, 0, 0:nrow]))
            nc.vector.tensor_scalar(hcols[:, :], cols[:, 2 * KD:nrow], 0.5, None, ALU.mult).then_inc(cols_ready, 1)

            def empty_turns(step, count):
                for i in range(count):
                    n = turn_of[step] + i
                    if n % 2 == 1:
                        ve.wait_ge(turn_full[1], n // 2 + 1)
                        o, src = turned_into(step, i)
                        nc.vector.tensor_copy(o, src).then_inc(turned[1], 1)

            norms = {}

            def moments(layer, p):
                norms[(layer, p)] = len(norms) + 1
                link(nc.vector.bn_stats(stats[:, layer, p, :], X[:, p, :]))
                nc.vector.bn_aggr(mv[:, layer, p, :], stats[:, layer, p, :]).then_inc(var_ready, 1)

            def normalize(layer, p):
                ve.wait_ge(rstd_ready, norms[(layer, p)])
                return nc.vector.tensor_scalar(X[:, p, :], X[:, p, :], mv[:, layer, p, 0:1], rstd[:, layer, p:p + 1],
                                               ALU.subtract, ALU.mult)

            for step in STEPS:
                kind = step[0]
                if kind == "xT":
                    p, n = step[1], turn_of[step]
                    if p >= 2 and n % 2 == 1:
                        m = work_of[("self_scores", p - 2)]
                        ve.wait_ge(work_full[m % 2], m // 2 + 1)
                    empty_turns(step, 1)
                    wait_turned(ve, n)
                    if p >= 2:
                        m = work_of[("self_scores", p - 2)]
                        ve.wait_ge(work_full[m % 2], m // 2 + 1)
                    nc.vector.tensor_tensor(kqT[:, p % 2], xT[:, p % 2],
                                            qkc[:, :].rearrange("p (h a) -> p h a", a=1).to_broadcast([P, H, P]),
                                            ALU.mult).then_inc(kq_ready, 1)
                elif kind in ("wqT", "x1T"):
                    empty_turns(step, 1)
                elif kind == "x2T":
                    if step[1] == 0:
                        ve.wait_ge(v1_in, 16)
                    empty_turns(step, 1)
                elif kind == "ctxT":
                    _, j, g = step
                    n = GROUPS * j + g
                    if n >= 2:
                        ve.wait_ge(scored, n - 1)
                    empty_turns(step, 2 * KD)
                elif kind == "pT":
                    if step[1] >= 1:
                        ve.wait_ge(attended, GROUPS * step[1])
                    empty_turns(step, GROUPS)
                elif kind == "self_scores":
                    p, n = step[1], work_of[step]
                    if p == 0:
                        ve.wait_ge(consts, 2)
                    ve.wait_ge(tanh_ready, p + 1)
                    nc.vector.scalar_tensor_tensor(
                        out=selfp[:, p % 2], in0=selfp[:, p % 2], scalar=1.0,
                        in1=mask[:, :].rearrange("p (a t) -> p a t", a=1).to_broadcast([P, H, P]),
                        op0=ALU.add, op1=ALU.mult).then_inc(selfp_ready, 1)
                elif kind == "self_out":
                    p, n = step[1], work_of[step]
                    ve.wait_ge(work_full[n % 2], n // 2 + 1)
                    ve.wait_ge(val_ready, p + 1)
                    nc.vector.tensor_tensor(X[:, p, :], psW[:, n % 2, :], X[:, p, :], ALU.add).then_inc(self_added, 1)
                    ve.wait_ge(self_added, p + 1)
                    moments(0, p)
                elif kind == "norm1":
                    normalize(0, step[1]).then_inc(x1_ready, 1)
                elif kind == "c":
                    p, n = step[1], work_of[step]
                    ve.wait_ge(work_full[n % 2], n // 2 + 1)
                    nc.vector.tensor_copy(c_sb[:, p:p + 1], psW[:, n % 2, 0:1]).then_inc(c_ready, 1)
                    if p == PAIRS - 1:
                        ve.wait_ge(c_ready, PAIRS)
                elif kind == "scores":
                    _, j, g = step
                    ve.wait_ge(scored, GROUPS * j + g + 1)
                    last = nc.vector.reduce_max(top[:, g:g + 1], psS[:, g, 0:GC], AX.X)
                    if g == GROUPS - 1:
                        link(last)
                elif kind == "softmax":
                    j = step[1]
                    link(nc.vector.reduce_max(topc[:, :], top[:, :], AX.X))
                    link(nc.vector.tensor_tensor(topc[:, :], topc[:, :], c_sb[:, j:j + 1], ALU.add))
                    link(nc.vector.tensor_tensor(topc[:, :], c_sb[:, j:j + 1], topc[:, :], ALU.subtract))
                    nc.vector.tensor_scalar(bias[:, :], topc[:, :], X_SCALE, None, ALU.mult).then_inc(bias_ready, 1)
                elif kind == "attend":
                    j = step[1]
                    ve.wait_ge(exp_ready, GROUPS * (j + 1))
                    link(nc.vector.reduce_sum(dsum[:, :], den[:, :], AX.X))
                    link(nc.vector.reciprocal(rden[:, :], dsum[:, :]))
                    ve.wait_ge(attended, GROUPS * (j + 1))
                    nc.vector.scalar_tensor_tensor(out=X[:, j, :], in0=psA[:, :], scalar=rden[:, :],
                                                   in1=X[:, j, :], op0=ALU.mult, op1=ALU.add).then_inc(att_added, 1)
                    ve.wait_ge(att_added, j + 1)
                    moments(1, j)
                elif kind == "norm2":
                    normalize(1, step[1]).then_inc(x2_ready, 1)
                elif kind == "ffn":
                    _, group, c = step
                    n, N, f = work_of[step], columns(group), piece(c)
                    i = FFN_COUNT[group] * FC + c
                    ve.wait_ge(gate_ready, i + 1)
                    link(nc.vector.scalar_tensor_tensor(out=tanh[0:f, i % 2, 0:N], in0=tanh[0:f, i % 2, 0:N],
                                                        scalar=1.0, in1=gate[0:f, i % 2, 0:N],
                                                        op0=ALU.add, op1=ALU.mult))
                    if c == 0 and FFN_COUNT[group] >= 1:
                        ve.wait_ge(summed, FFN_COUNT[group])
                    nc.vector.scalar_tensor_tensor(out=act[0:f, c, 0:N], in0=psW[0:f, n % 2, 256:256 + N],
                                                   scalar=cols[0:f, 2 * KD + FC + c:2 * KD + FC + c + 1],
                                                   in1=tanh[0:f, i % 2, 0:N],
                                                   op0=ALU.add, op1=ALU.mult).then_inc(act_ready, 1)
                elif kind == "ffn_out":
                    for i, p in enumerate(step[1]):
                        n = work_of[step] + i
                        ve.wait_ge(work_full[n % 2], n // 2 + 1)
                        ve.wait_ge(x2b_ready, p + 1)
                        nc.vector.tensor_tensor(X[:, p, :], psW[:, n % 2, :], X[:, p, :], ALU.add).then_inc(y_added, 1)
                        ve.wait_ge(y_added, p + 1)
                        moments(2, p)
                        normalize(2, p).then_inc(y_ready, 1)


_INS = ['x', 'ctx_4096', 'L0_attn_bv_q', 'L0_attn_bv_k', 'L0_attn_bv_v', 'L0_xattn_Wq', 'L0_xattn_bq', 'L0_xattn_Wk',
        'L0_xattn_bk', 'L0_ffn_U1', 'L0_ffn_V1', 'L0_ffn_U2', 'L0_ffn_V2', 'L0_ffn_b1', 'L0_ffn_b2']


def kernel(**inputs):
    import numpy as _np
    import concourse.bacc as _bacc
    from concourse import mybir as _mybir
    from concourse.bass_utils import run_bass_kernel_spmd as _run

    nc = _bacc.Bacc("TRN2", target_bir_lowering=False, num_devices=1)
    arrays, args = {}, []
    for name in _INS:
        a = _np.ascontiguousarray(inputs[name])
        arrays[f"in_{name}_dram"] = a
        args.append(nc.dram_tensor(f"in_{name}_dram", a.shape, _mybir.dt.from_np(a.dtype), kind="ExternalInput").ap())
    shape = inputs['x'].shape
    out = nc.dram_tensor("out_dram", shape, _mybir.dt.from_np(_np.dtype('float32')), kind="ExternalOutput").ap()
    decoder_layer(nc, *args, out)
    r = _run(nc, [arrays], core_ids=[0])
    return r.results[0]["out_dram"]
```

```python
from contextlib import ExitStack

import concourse.bass as bass
from concourse import mybir

F32 = mybir.dt.float32
ALU = mybir.AluOpType
ACT = mybir.ActivationFunctionType
AX = mybir.AxisListType

P = 128
EPS = 1e-5



LAG = 3


def steps(pairs, groups, chunks):
    last = groups - 1
    out = [("xT", 0), ("xT", 1), ("bind",), ("self_scores", 0), ("xT", 2), ("self_scores", 1), ("self_out", 0),
           ("xT", 3), ("self_scores", 2), ("self_out", 1), ("norm1", 0), ("self_scores", 3), ("ctxT", 0, 0, 0),
           ("self_out", 2), ("norm1", 1), ("x1T", 0), ("ctxT", 0, 0, 1), ("self_out", 3), ("norm1", 2),
           ("x1T", 1), ("wqT", 0), ("wqT", 1), ("norm1", 3), ("x1T", 2), ("wqT", 2), ("wqT", 3), ("columns",),
           ("ctxT", 0, 1, 0), ("x1T", 3), ("ctxT", 0, 1, 1)]
    out += [("q", m) for m in range(4)]
    for m in range(4):
        out += [("g", m), ("c", m)]
    for j in range(pairs):
        out.append(("scores", j, 0))
        if j == 0:
            out += [("ctxT", j, last, 0), ("ctxT", j, last, 1)]
        else:
            out += [("cross", j, last, 0), ("cross", j, last, 1), ("norm2", j - 1)]
        out += [("scores", j, g) for g in range(1, groups)]
        out.append(("bias", j))
        if j > 0:
            out.append(("x2T", j - 1))
        if j + 1 < pairs:
            halves = [("ctxT", j + 1, 0, h) for h in range(2)]
        else:
            halves = [("ffn", (0, 1), c) for c in range(chunks)]
            out.append(("proj", (0, 1)))
        for g in range(groups):
            out += halves[g:g + 1] + [("exp", j, g)]
            if g == 0 and j + 1 < pairs:
                out.append(("cross", j + 1, 1, 0))
        out += halves[groups:]
        if j + 1 == pairs:
            out += [("ffn_sum", (0, 1)), ("pT", j), ("ffn_out", (0, 1)), ("proj", (2,)), ("norm3", 0), ("norm3", 1)]
        else:
            out += [("pT", j), ("cross", j + 1, 1, 1)]
        out.append(("attend", j))
    out += [("ffn", (2,), c) for c in range(5)] + [("norm2", 3), ("ffn", (2,), 5), ("x2T", 3)]
    out += [("ffn", (2,), c) for c in range(6, chunks)] + [("ffn_sum", (2,)), ("proj", (3,))]
    out += [("ffn", (3,), 0), ("ffn", (3,), 1), ("ffn_out", (2,))] + [("ffn", (3,), c) for c in range(2, 6)]
    out += [("norm3", 2)] + [("ffn", (3,), c) for c in range(6, chunks)]
    out += [("ffn_sum", (3,)), ("ffn_out", (3,)), ("norm3", 3)]
    return out


def decoder_layer(nc, x, ctx, bv_q, bv_k, bv_v, Wq, bq, Wk, bk, U1, V1, U2, V2, b1, b2, out):
    B, T, D = x.shape
    S = ctx.shape[1]
    H, HD = bv_q.shape
    R = U1.shape[1]
    INTER = U2.shape[0]
    PAIRS = B // 2
    TP = P // 2
    KD = D // P
    KT = 12
    Q = S // KT
    GROUPS = 3
    KG = KT // GROUPS
    GC = KG * Q
    BL = 32
    NB = -(-GC // BL)
    BR = P // BL
    FC = -(-INTER // P)
    FT = INTER - (FC - 1) * P
    RING = 5
    SLOTS = 4
    SELF_SCALE = 4.0 * float(HD) ** -0.5
    X_SCALE = float(D) ** -0.5
    QA = 112
    assert D == 512 and HD == P and H == KD and R == P and Q * KT == S and Q <= P and GC <= 512
    assert PAIRS == 4 and T <= TP

    STEPS = steps(PAIRS, GROUPS, FC)

    es = ExitStack()
    with es:
        def sb(name, shape):
            return es.enter_context(nc.sbuf_tensor(name, shape, F32))

        def ps(name, shape):
            return es.enter_context(nc.psum_tensor(name, shape, F32))

        def sem(name):
            return es.enter_context(nc.semaphore(name))

        ctx_sb = sb("ctx_sb", [P, SLOTS, KT, D])
        ctxT = sb("ctxT", [P, 2, 2, KD, NB * BL])
        prob = sb("prob", [P, KT, Q])
        probT = sb("probT", [P, KT, P])
        X = sb("X", [P, PAIRS, D])
        gT = sb("gT", [P, KD, B, TP])
        u2 = sb("u2", [P, FC, R])
        b2_rows = sb("b2_rows", [P, D])
        shared = sb("shared", [P, 8192 + KD * B * T])
        wkv = shared[:, 0:2048].rearrange("p (k x) -> p k x", k=KD)
        wqT = shared[:, 2048:4096].rearrange("p (k x) -> p k x", k=KD)
        qT = shared[:, 4096:6144].rearrange("p (k b t) -> p k b t", k=KD, b=B)
        x1T = shared[:, 6144:6144 + KD * B * T].rearrange("p (k b t) -> p k b t", k=KD, b=B)
        NMAX = 4 * T
        v1 = shared[:, 0:2 * INTER]
        at = 2 * INTER
        x2T = shared[:, at:at + KD * B * T].rearrange("p (k n) -> p k n", k=KD)
        at += KD * B * T
        u1 = shared[:, at:at + KD * R].rearrange("p (k r) -> p k r", k=KD)
        at += KD * R
        v2 = shared[:, at:at + D]
        at += D
        blocks = shared[:, at:at + 2 * NB * P].rearrange("p (a n x) -> p a n x", a=2, n=NB)
        assert at + 2 * NB * P <= 8192 + KD * B * T
        prT = shared[:, at:at + NMAX]
        at += NMAX
        act = shared[:, at:at + FC * NMAX].rearrange("p (c n) -> p c n", c=FC)
        at += FC * NMAX
        gate = shared[:, at:at + 2 * NMAX].rearrange("p (a n) -> p a n", a=2)
        at += 2 * NMAX
        tanh = shared[:, at:at + 2 * NMAX].rearrange("p (a n) -> p a n", a=2)
        at += 2 * NMAX
        assert at <= 8192 + KD * B * T
        zT = sb("zT", [P, 2, 2, TP])
        early = ctx_sb[:, SLOTS - 1].rearrange("p k x -> p (k x)")
        wq = early[:, 0:2048].rearrange("p (k x) -> p k x", k=KD)
        xT = early[:, 2048:3072].rearrange("p (a h t) -> p a h t", a=2, h=H)
        kqT = early[:, 3072:4096].rearrange("p (a h t) -> p a h t", a=2, h=H)
        selfp = early[:, 4096:5120].rearrange("p (a h t) -> p a h t", a=2, h=H)
        val = early[:, 5120:6144].rearrange("p (a n) -> p a n", a=2)

        ident = sb("ident", [P, P])
        mask = sb("mask", [P, P])
        NROW = 2 * KD + 2 * FC
        start = prob[:, :, :].rearrange("p k q -> p (k q)")
        vdiag = start[0:H, 0:D].rearrange("p (h d) -> p h d", h=H)
        ones = start[0:H, D + 3 * P:D + 4 * P]
        rows = start[0:NROW, D + 4 * P:D + 5 * P]
        bv = probT[0:3 * H, H, :]
        sign = probT[0:3 * H, H + 1, :]
        bound = probT[0:3 * H, H + 2, :]
        v_rows = probT[:, 0:H, :].rearrange("p h d -> p (h d)")
        cols = sb("cols", [P, 2 * KD + 2 * FC])
        hcols = sb("hcols", [P, 2 * FC])
        asum = sb("asum", [3 * H, 1])
        bcols = sb("bcols", [P, 3 * H])
        qkc = sb("qkc", [P, H])
        c_sb = sb("c_sb", [P, PAIRS])
        top = sb("top", [P, GROUPS])
        topc = sb("topc", [P, 1])
        bias = sb("bias", [P, 1])
        den = sb("den", [P, GROUPS])
        dsum = sb("dsum", [P, 1])
        rden = sb("rden", [P, 1])
        stats = sb("stats", [P, 3, PAIRS, 6])
        mv = sb("mv", [P, 3, PAIRS, 2])
        veps = sb("veps", [P, 3, PAIRS])
        rstd = sb("rstd", [P, 3, PAIRS])
        mhalf = sb("mhalf", [P, 1])

        psS = ps("psS", [P, GROUPS, 512])
        ring = ps("ring", [P, RING, 512])
        psA = psS[:, GROUPS - 1]
        psZ = psS[:, 0]

        x_in = [sem("x_in01"), sem("x_in2"), sem("x_in3")]
        bv_in, rows_in, b2_in = sem("bv_in"), sem("rows_in"), sem("b2_in")
        wq_in, wk_in, v1_in, u_in = sem("wq_in"), sem("wk_in"), sem("v1_in"), sem("u_in")
        ctx_in = [[sem(f"ctx_in{s}_{g}") for g in range(GROUPS)] for s in range(SLOTS)]
        rows_zero = sem("rows_zero")
        consts = sem("consts")
        pool_chain = sem("pool_chain")
        dve_chain = sem("dve_chain")
        bound_ready = sem("bound_ready")
        qkc_ready = sem("qkc_ready")
        vdiag_ready = sem("vdiag_ready")
        cols_ready = sem("cols_ready")
        v_rows_ready = sem("v_rows_ready")
        kq_ready = sem("kq_ready")
        val_ready = sem("val_ready")
        tanh_ready = sem("tanh_ready")
        selfp_ready = sem("selfp_ready")
        var_ready = sem("var_ready")
        rstd_ready = sem("rstd_ready")
        x1_ready = sem("x1_ready")
        x2_ready = sem("x2_ready")
        x2b_ready = sem("x2b_ready")
        q_ready, c_ready, g_ready = sem("q_ready"), sem("c_ready"), sem("g_ready")
        blocks_in = [sem("blocks_in0"), sem("blocks_in1")]
        crossed = sem("crossed")
        scored = sem("scored")
        bias_ready = sem("bias_ready")
        exp_ready = sem("exp_ready")
        attended = sem("attended")
        turn_full = [sem("turn_full_act"), sem("turn_full_dve")]
        turned = [sem("turned_act"), sem("turned_dve")]
        worked = sem("worked")
        v_bound = sem("v_bound")
        summed = sem("summed")
        self_added = sem("self_added")
        att_added = sem("att_added")
        y_added = sem("y_added")
        pr_ready = sem("pr_ready")
        gate_ready = sem("gate_ready")
        act_ready = sem("act_ready")
        z_ready = sem("z_ready")
        y_ready = sem("y_ready")
        out_sem = sem("out_sem")

        FFN_COUNT = {g: i for i, g in enumerate(((0, 1), (2,), (3,)))}
        turn_of, work_of = {}, {}
        turn_bank, work_bank = [], []
        turn_by = []
        by_engine = [0, 0]
        job_read = []
        for s in STEPS:
            kind = s[0]
            turns = {"xT": 1, "wqT": 1, "x1T": 1, "x2T": 1, "ctxT": KD, "pT": GROUPS}.get(kind, 0)
            if turns:
                turn_of[s] = len(turn_bank)
                for i in range(turns):
                    e = i % 2 if kind in ("ctxT", "pT") else 0
                    by_engine[e] += 1
                    turn_by.append((e, by_engine[e]))
                    turn_bank.append(len(job_read) % RING)
                    job_read.append((kq_ready, H * (s[1] + 1)) if kind == "xT" else (turned[e], by_engine[e]))
            read = {"bind": qkc_ready, "columns": cols_ready, "self_scores": tanh_ready, "self_out": self_added, "q": q_ready, "c": c_ready,
                    "g": g_ready, "proj": pr_ready, "ffn": act_ready, "ffn_out": y_added}.get(kind)
            if read is not None:
                work_of[s] = len(work_bank)
                if kind == "proj":
                    done = [FFN_COUNT[s[1]] + 1]
                elif kind == "ffn":
                    done = [FFN_COUNT[s[1]] * FC + s[2] + 1]
                elif kind == "ffn_out":
                    done = [p + 1 for p in s[1]]
                elif kind in ("bind", "columns"):
                    done = [1]
                else:
                    done = [s[1] + 1]
                for d in done:
                    work_bank.append(len(job_read) % RING)
                    job_read.append((read, d))

        def turn(n):
            return ring[:, turn_bank[n]]

        def work(n):
            return ring[:, work_bank[n]]

        def wait_turned(eng, first, count=1):
            for e in range(2):
                counts = [c for by, c in turn_by[first:first + count] if by == e]
                if counts:
                    eng.wait_ge(turned[e], counts[-1])

        def wait_turn_full(eng, n):
            e, count = turn_by[n]
            eng.wait_ge(turn_full[e], count)

        def turned_into(step, i):
            n = turn_of[step] + i
            bank = turn(n)
            kind = step[0]
            if kind == "xT":
                return xT[:, step[1] % 2], bank.rearrange("p (h t) -> p h t", h=H)
            if kind == "wqT":
                m = step[1]
                return wqT[:, :, m * P:(m + 1) * P], bank.rearrange("p (k t) -> p k t", k=KD)
            if kind in ("x1T", "x2T"):
                src = bank.rearrange("p (k b t) -> p k b t", k=KD, b=2)[:, :, :, 0:T]
                p = step[1]
                if kind == "x1T":
                    return x1T[:, :, 2 * p:2 * p + 2, :], src
                return x2T[:, :, 2 * T * p:2 * T * (p + 1)].rearrange("p k (b t) -> p k b t", b=2), src
            if kind == "ctxT":
                _, j, g, h = step
                return ctxT[:, (GROUPS * j + g) % 2, h, i, 0:GC], bank[:, 0:GC]
            return probT[0:Q, KG * i:KG * i + KG, :], bank[0:Q].rearrange("p (k t) -> p k t", k=KG)

        def spread(row, piece):
            return row.rearrange("p (x k) -> p k x", k=KD)[:, piece]

        def columns(group):
            return len(group) * 2 * T

        def wait_x(eng, p):
            if p < 2:
                eng.wait_ge(x_in[0], 32)
            else:
                eng.wait_ge(x_in[1], 32)
            if p == 3:
                eng.wait_ge(x_in[2], 32)

        def wait_ctx(eng, b, g):
            eng.wait_ge(ctx_in[b % SLOTS][g], 32 * (b // SLOTS + 1))

        CROSS = [s for s in STEPS if s[0] == "cross"]

        def piece(c):
            return P if c < FC - 1 else FT

        block = es.enter_context(nc.Block())

        @block.sync
        def _(sp):
            def load_x(h, p0, count, rows_):
                src = bass.AP(tensor=x.tensor, offset=(2 * p0 + h) * T * D,
                              ap=[[D, rows_], [2 * T * D, count], [1, D]])
                sp.dma_start(X[h * TP:h * TP + rows_, p0:p0 + count, :], src).then_inc(x_in[p0 // 2 + p0 // 3], 16)

            load_x(0, 0, 2, TP)
            load_x(1, 0, 2, TP)
            load_x(0, 2, 2, TP)
            load_x(1, 2, 1, TP)
            load_x(1, 3, 1, T)
            sp.dma_start(X[TP + T:P, PAIRS - 1, :], x[0, 0:TP - T, :]).then_inc(x_in[2], 16)

            def load_ctx(b, g):
                slot = b % SLOTS
                if b >= SLOTS:
                    sp.wait_ge(attended, GROUPS * (b // 2 - SLOTS // 2) + g + 1)
                v = ctx[b, GC * g:GC * g + GC].rearrange("(q k) x -> q k x", k=KG)
                ks = slice(KG * g, KG * g + KG)
                for q0, q1 in ((0, QA), (QA, Q)):
                    sp.dma_start(ctx_sb[q0:q1, slot, ks, :], v[q0:q1]).then_inc(ctx_in[slot][g], 16)

            def load_blocks(step):
                _, j, g, h = step
                i = CROSS.index(step)
                if i >= 2:
                    sp.wait_ge(crossed, KD * (i - 1))
                row = (2 * j + h) * S + GC * g
                full = NB if step != CROSS[-1] else NB - 1
                for r in range(BR):
                    src = bass.AP(tensor=ctx.tensor, offset=row * D + P * r, ap=[[D, BL], [BL * D, full], [1, P]])
                    sp.dma_start(blocks[BL * r:BL * r + BL, h, 0:full, :], src).then_inc(blocks_in[h], 16)
                if full < NB:
                    left = GC - full * BL
                    src = ctx[2 * j + h, S - left:S].rearrange("r (i x) -> i r x", x=P)
                    for r in range(BR):
                        sp.dma_start(blocks[BL * r:BL * r + left, h, full, :], src[r]).then_inc(blocks_in[h], 16)

            for g in range(GROUPS):
                for b in range(2):
                    load_ctx(b, g)
                if g == 0:
                    sp.dma_start(wq, Wq.rearrange("(k p) x -> p k x", p=P)).then_inc(wq_in, 16)
                    sp.wait_ge(rows_zero, 1)
                    sp.dma_start(rows[0:KD, :], bq.rearrange("(k p) -> k p", p=P)).then_inc(rows_in, 16)
                    sp.dma_start(rows[KD:2 * KD, :], bk.rearrange("(k p) -> k p", p=P)).then_inc(rows_in, 16)
                    for h in range(2):
                        r, o = 2 * KD + h * FC, h * INTER
                        sp.dma_start(rows[r:r + FC - 1, :], b1[o:o + (FC - 1) * P].rearrange("(k p) -> k p", p=P))\
                          .then_inc(rows_in, 16)
                        sp.dma_start(rows[r + FC - 1:r + FC, 0:FT],
                                     b1[o + (FC - 1) * P:o + INTER].rearrange("(a p) -> a p", a=1)).then_inc(rows_in, 16)
                if g == 1:
                    sp.dma_start(wkv, Wk.rearrange("(k p) x -> p k x", p=P)).then_inc(wk_in, 16)
                    sp.dma_start(b2_rows[:, :], b2.rearrange("(a n) -> a n", a=1).to_broadcast([P, D])).then_inc(b2_in, 16)
            n = work_of[("self_out", PAIRS - 1)]
            for g in range(GROUPS):
                load_ctx(2, g)
                if g == 0:
                    sp.wait_ge(worked, n + 1)
                    n = turn_of[("wqT", KD - 1)]
                    wait_turn_full(sp, n)
                load_ctx(3, g)
            sp.dma_start(u2[:, 0:FC - 1, :], U2[0:(FC - 1) * P].rearrange("(c p) r -> p c r", p=P)).then_inc(u_in, 16)
            sp.dma_start(u2[0:FT, FC - 1, :], U2[(FC - 1) * P:INTER]).then_inc(u_in, 16)
            n = work_of[("c", PAIRS - 1)]
            sp.wait_ge(worked, n + 1)
            load_blocks(CROSS[0])
            load_blocks(CROSS[1])
            sp.dma_start(v1, V1).then_inc(v1_in, 16)
            sp.dma_start(u1, U1.rearrange("(k p) r -> p k r", p=P)).then_inc(u_in, 16)
            sp.dma_start(v2, V2).then_inc(u_in, 16)
            load_blocks(CROSS[2])
            load_blocks(CROSS[3])
            for j in range(SLOTS // 2, PAIRS):
                for g in range(GROUPS - 1):
                    load_ctx(2 * j, g)
                    load_ctx(2 * j + 1, g)
                load_blocks(CROSS[4 * j - 4])
                load_blocks(CROSS[4 * j - 3])
                load_ctx(2 * j, GROUPS - 1)
                load_ctx(2 * j + 1, GROUPS - 1)
                load_blocks(CROSS[4 * j - 2])
                load_blocks(CROSS[4 * j - 1])
            for p in range(PAIRS):
                sp.wait_ge(y_ready, p + 1)
                for h in range(2):
                    sp.dma_start(out[2 * p + h], X[h * TP:h * TP + T, p, :]).then_inc(out_sem, 16)
            sp.wait_ge(out_sem, 16 * B)

        @block.gpsimd
        def _(pool):
            chained = [0]

            def link(ins):
                chained[0] += 1
                ins.then_inc(pool_chain, 1)
                pool.wait_ge(pool_chain, chained[0])

            link(nc.gpsimd.memset(ident[:, :], 0.0))
            nc.gpsimd.affine_select(out=ident[:, :], in_=ident[:, :], compare_op=ALU.not_equal, fill=1.0,
                                    base=0, pattern=[[-1, P]], channel_multiplier=1).then_inc(consts, 1)
            nc.gpsimd.memset(ones[:, :], 1.0)
            nc.gpsimd.memset(mhalf[:, :], -0.5)
            link(nc.gpsimd.memset(mask[:, :], 0.5))
            link(nc.gpsimd.affine_select(out=mask[:, :], in_=mask[:, :], compare_op=ALU.is_ge, fill=0.0,
                                         base=0, pattern=[[1, P]], channel_multiplier=-1))
            nc.gpsimd.memset(mask[0:TP, TP:P], 0.0).then_inc(consts, 1)
            pool.wait_ge(bound_ready, 1)
            nc.gpsimd.affine_select(out=vdiag[:, :, :], in_=probT[0:H, H:H + 1, :].to_broadcast([H, H, P]),
                                    compare_op=ALU.is_equal, fill=0.0, base=0,
                                    pattern=[[-1, H], [0, P]], channel_multiplier=1).then_inc(vdiag_ready, 1)
            nc.gpsimd.memset(qT[:, :, :, T:TP], 0.0)
            nc.gpsimd.memset(gT[:, :, :, T:TP], 0.0)
            nc.gpsimd.memset(zT[:, :, :, T:TP], 0.0).then_inc(consts, 1)
            pool.wait_ge(v_rows_ready, 1)
            norms = 0

            def inverse_deviation(layer, p):
                nonlocal norms
                norms += 1
                pool.wait_ge(var_ready, norms)
                link(nc.gpsimd.tensor_scalar(veps[:, layer, p:p + 1], mv[:, layer, p, 1:2], EPS, None, ALU.add))
                nc.gpsimd.tensor_tensor(rstd[:, layer, p:p + 1], veps[:, layer, p:p + 1], mhalf[:, :],
                                        ALU.pow).then_inc(rstd_ready, 1)

            for step in STEPS:
                kind = step[0]
                if kind == "xT":
                    p = step[1]
                    wait_x(pool, p)
                    if p >= 2:
                        n = work_of[("self_out", p - 2)]
                        pool.wait_ge(worked, n + 1)
                    nc.gpsimd.tensor_tensor(val[:, p % 2, :], X[:, p, :], v_rows[:, :],
                                            ALU.mult).then_inc(val_ready, 1)
                elif kind == "self_out":
                    inverse_deviation(0, step[1])
                elif kind == "attend":
                    inverse_deviation(1, step[1])
                elif kind == "ffn_out":
                    for p in step[1]:
                        inverse_deviation(2, p)
                elif kind == "x2T":
                    p = step[1]
                    n = turn_of[step]
                    pool.wait_ge(b2_in, 16)
                    wait_turn_full(pool, n)
                    nc.gpsimd.tensor_tensor(X[:, p, :], X[:, p, :], b2_rows[:, :], ALU.add).then_inc(x2b_ready, 1)

        @block.scalar
        def _(sc):
            for i, src in enumerate((bv_v, bv_q, bv_k)):
                sc.dma_start(bv[i * H:(i + 1) * H, :], src).then_inc(bv_in, 16)
            nc.scalar.preload_act_table(ACT.Tanh)

            def empty_turns(step, count):
                for i in range(count):
                    n = turn_of[step] + i
                    if turn_by[n][0] == 0:
                        wait_turn_full(sc, n)
                        o, src = turned_into(step, i)
                        nc.scalar.activation(o, src, ACT.Copy).then_inc(turned[0], 1)

            for step in STEPS:
                kind = step[0]
                if kind == "xT":
                    p = step[1]
                    if p >= 2:
                        n = work_of[("self_scores", p - 2)]
                        sc.wait_ge(worked, n + 1)
                    empty_turns(step, 1)
                    if p == 0:
                        sc.wait_ge(qkc_ready, 1)
                    for h in range(H):
                        nc.scalar.activation(kqT[:, p % 2, h, :], turn(turn_of[step])[:, h * P:(h + 1) * P],
                                             ACT.Copy, scale=qkc[:, h:h + 1]).then_inc(kq_ready, 1)
                elif kind == "bind":
                    sc.wait_ge(v_bound, 1)
                    nc.scalar.activation(v_rows[:, :], psA[:, :], ACT.Copy).then_inc(v_rows_ready, 1)
                elif kind in ("wqT", "x1T"):
                    empty_turns(step, 1)
                elif kind == "x2T":
                    if step[1] == 0:
                        sc.wait_ge(v1_in, 16)
                    empty_turns(step, 1)
                elif kind == "ctxT":
                    _, j, g, h = step
                    n = GROUPS * j + g
                    if n >= 2 and h == 0:
                        sc.wait_ge(scored, n - 1)
                    empty_turns(step, KD)
                elif kind == "pT":
                    if step[1] >= 1:
                        sc.wait_ge(attended, GROUPS * step[1])
                    empty_turns(step, GROUPS)
                elif kind == "self_scores":
                    p, n = step[1], work_of[step]
                    sc.wait_ge(worked, n + 1)
                    if p >= 2:
                        m = work_of[("self_out", p - 2)]
                        sc.wait_ge(worked, m + 1)
                    nc.scalar.activation(selfp[:, p % 2], work(n).rearrange("p (h t) -> p h t", h=H),
                                         ACT.Tanh, scale=0.5 * SELF_SCALE).then_inc(tanh_ready, 1)
                elif kind == "q":
                    m, n = step[1], work_of[step]
                    sc.wait_ge(worked, n + 1)
                    if m == 0:
                        sc.wait_ge(consts, 3)
                        sc.wait_ge(cols_ready, 1)
                    nc.scalar.activation(qT[:, m, :, 0:T],
                                         work(n)[:, 0:B * T].rearrange("p (b t) -> p b t", b=B),
                                         ACT.Identity, bias=cols[:, m:m + 1]).then_inc(q_ready, 1)
                elif kind == "g":
                    m, n = step[1], work_of[step]
                    sc.wait_ge(worked, n + 1)
                    nc.scalar.activation(gT[:, m, :, 0:T],
                                         work(n)[:, 0:B * T].rearrange("p (b t) -> p b t", b=B),
                                         ACT.Copy).then_inc(g_ready, 1)
                elif kind == "exp":
                    _, j, g = step
                    if g == 0:
                        sc.wait_ge(bias_ready, j + 1)
                    if g == 0 and j >= 1:
                        wait_turn_full(sc, turn_of[("pT", j - 1)] + GROUPS - 1)
                        wait_turn_full(sc, turn_of[("pT", j - 1)] + GROUPS - 2)
                    order = "p (q k) -> p k q" if ("cross", j, g, 0) in CROSS else "p (k q) -> p k q"
                    nc.scalar.activation(prob[:, KG * g:KG * g + KG, :],
                                         psS[:, g, 0:GC].rearrange(order, k=KG),
                                         ACT.Exp, bias=bias[:, :], scale=X_SCALE,
                                         accum_out=den[:, g:g + 1]).then_inc(exp_ready, 1)
                elif kind == "proj":
                    n, N = work_of[step], columns(step[1])
                    if step[1][0] == 0:
                        sc.wait_ge(crossed, KD * len(CROSS))
                    sc.wait_ge(worked, n + 1)
                    nc.scalar.activation(prT[:, 0:N], work(n)[:, 0:N], ACT.Copy).then_inc(pr_ready, 1)
                elif kind == "ffn":
                    _, group, c = step
                    n, N, f = work_of[step], columns(group), piece(step[2])
                    i = FFN_COUNT[group] * FC + c
                    sc.wait_ge(worked, n + 1)
                    if i >= 2:
                        sc.wait_ge(act_ready, i - 1)
                    nc.scalar.activation(tanh[0:f, i % 2, 0:N], work(n)[0:f, 0:N], ACT.Tanh,
                                         bias=hcols[0:f, c:c + 1], scale=0.5)
                    nc.scalar.activation(gate[0:f, i % 2, 0:N], work(n)[0:f, 0:N], ACT.Identity,
                                         bias=cols[0:f, 2 * KD + c:2 * KD + c + 1]).then_inc(gate_ready, 1)
                elif kind == "ffn_sum":
                    group = step[1]
                    sc.wait_ge(summed, FFN_COUNT[group] + 1)
                    nc.scalar.activation(zT[:, 0:len(group), :, 0:T],
                                         psZ[:, 0:columns(group)].rearrange("p (a b t) -> p a b t", b=2, t=T),
                                         ACT.Copy, scale=0.5).then_inc(z_ready, 1)

        @block.tensor
        def _(pe):
            jobs = [0]

            def next_bank():
                if jobs[0] >= RING:
                    pe.wait_ge(*job_read[jobs[0] - RING])
                jobs[0] += 1
                return ring[:, (jobs[0] - 1) % RING]

            pe.wait_ge(consts, 1)

            def inner_sum(group, c):
                i, N, f = FFN_COUNT[group] * FC + c, columns(group), piece(c)
                pe.wait_ge(act_ready, i + 1)
                if c == 0:
                    if FFN_COUNT[group] == 0:
                        pe.wait_ge(exp_ready, GROUPS * (PAIRS - 1) + 1)
                    else:
                        pe.wait_ge(z_ready, FFN_COUNT[group])
                mm = pe.matmul(psZ[:, 0:N], u2[0:f, c, :], act[0:f, c, 0:N], start=(c == 0), stop=(c == FC - 1))
                if c == FC - 1:
                    mm.then_inc(summed, 1)

            for step in STEPS:
                kind = step[0]
                if kind == "xT":
                    p, n = step[1], turn_of[step]
                    wait_x(pe, p)
                    bank = next_bank()
                    for h in range(H):
                        mm = pe.transpose(bank[:, h * P:(h + 1) * P], X[:, p, h * P:(h + 1) * P], ident[:, :])
                    mm.then_inc(turn_full[turn_by[n][0]], 1)
                elif kind == "bind":
                    bank = next_bank()
                    pe.wait_ge(bound_ready, 1)
                    pe.transpose(bank[:, 0:3 * H], bv, ident[0:3 * H, 0:3 * H]).then_inc(worked, 1)
                    pe.wait_ge(vdiag_ready, 1)
                    pe.matmul(psA, ones, vdiag.rearrange("k h d -> k (h d)"), start=True, stop=True).then_inc(v_bound, 1)
                elif kind == "columns":
                    bank = next_bank()
                    pe.wait_ge(rows_in, 16 * 6)
                    pe.transpose(bank[:, 0:NROW], rows, ident[0:NROW, 0:NROW]).then_inc(worked, 1)
                elif kind == "self_scores":
                    p, n = step[1], work_of[step]
                    bank = next_bank()
                    pe.wait_ge(kq_ready, H * (p + 1))
                    for h in range(H):
                        mm = pe.matmul(bank[:, h * P:(h + 1) * P], kqT[:, p % 2, h, :], xT[:, p % 2, h, :],
                                       start=True, stop=True)
                    mm.then_inc(worked, 1)
                elif kind == "self_out":
                    p, n = step[1], work_of[step]
                    bank = next_bank()
                    pe.wait_ge(selfp_ready, p + 1)
                    pe.wait_ge(val_ready, p + 1)
                    for h in range(H):
                        mm = pe.matmul(bank[:, h * P:(h + 1) * P], selfp[:, p % 2, h, :],
                                       val[:, p % 2, h * P:(h + 1) * P], start=True, stop=True)
                    mm.then_inc(worked, 1)
                elif kind == "wqT":
                    m, n = step[1], turn_of[step]
                    if m == 0:
                        pe.wait_ge(wq_in, 16)
                    bank = next_bank()
                    for k in range(KD):
                        mm = pe.transpose(bank[:, k * P:(k + 1) * P], wq[:, m, k * P:(k + 1) * P], ident[:, :])
                    mm.then_inc(turn_full[turn_by[n][0]], 1)
                elif kind in ("x1T", "x2T"):
                    p, n = step[1], turn_of[step]
                    pe.wait_ge(x1_ready if kind == "x1T" else x2_ready, p + 1)
                    bank = next_bank()
                    for k in range(KD):
                        mm = pe.transpose(bank[:, k * P:(k + 1) * P], X[:, p, k * P:(k + 1) * P], ident[:, :])
                    mm.then_inc(turn_full[turn_by[n][0]], 1)
                elif kind == "q":
                    m, n = step[1], work_of[step]
                    if m == 0:
                        wait_turned(pe, turn_of[("x1T", PAIRS - 2)], 1)
                        wait_turned(pe, turn_of[("x1T", PAIRS - 1)], 1)
                    bank = next_bank()
                    for k in range(KD):
                        mm = pe.matmul(bank[:, 0:B * T], wqT[:, k, m * P:(m + 1) * P],
                                       x1T[:, k, :, :].rearrange("p b t -> p (b t)"), start=(k == 0), stop=(k == KD - 1))
                    mm.then_inc(worked, 1)
                elif kind == "c":
                    p, n = step[1], work_of[step]
                    bank = next_bank()
                    for k in range(KD):
                        mm = pe.matmul(bank[:, 0:1], qT[:, k, 2 * p:2 * p + 2, :].rearrange("p b t -> p (b t)"),
                                       cols[:, KD + k:KD + k + 1], start=(k == 0), stop=(k == KD - 1))
                    mm.then_inc(worked, 1)
                elif kind == "g":
                    m, n = step[1], work_of[step]
                    if m == 0:
                        pe.wait_ge(wk_in, 16)
                    bank = next_bank()
                    for k in range(KD):
                        if m == 0:
                            pe.wait_ge(q_ready, k + 1)
                        mm = pe.matmul(bank[:, 0:B * T], spread(wkv[:, k, :], m), qT[:, k, :, 0:T],
                                       start=(k == 0), stop=(k == KD - 1))
                    mm.then_inc(worked, 1)
                elif kind == "ctxT":
                    _, j, g, h = step
                    b = 2 * j + h
                    wait_ctx(pe, b, g)
                    for kd in range(KD):
                        n = turn_of[step] + kd
                        bank = next_bank()
                        for k in range(KG):
                            mm = pe.transpose(bank[:, k * Q:(k + 1) * Q],
                                              spread(ctx_sb[0:Q, b % SLOTS, KG * g + k, :], kd),
                                              ident[0:Q, 0:Q])
                        mm.then_inc(turn_full[turn_by[n][0]], 1)
                elif kind == "scores":
                    _, j, g = step
                    if j == 0 and g == 0:
                        pe.wait_ge(g_ready, KD)
                    if j >= 1:
                        pe.wait_ge(exp_ready, GROUPS * (j - 1) + g + 1)
                        if g == GROUPS - 1:
                            pe.wait_ge(att_added, j)
                    by_blocks = ("cross", j, g, 0) in CROSS
                    if not by_blocks:
                        wait_turned(pe, turn_of[("ctxT", j, g, 0)], KD)
                        wait_turned(pe, turn_of[("ctxT", j, g, 1)], KD)
                    for kd in range(KD):
                        for h in range(2):
                            if by_blocks:
                                pe.wait_ge(crossed, KD * CROSS.index(("cross", j, g, h)) + kd + 1)
                            mm = pe.matmul(psS[h * TP:(h + 1) * TP, g, 0:GC], gT[:, kd, 2 * j + h, :],
                                           ctxT[:, (GROUPS * j + g) % 2, h, kd, 0:GC],
                                           start=(kd == 0), stop=(kd == KD - 1))
                    mm.then_inc(scored, 1)
                elif kind == "pT":
                    j = step[1]
                    for g in range(GROUPS):
                        n = turn_of[step] + g
                        pe.wait_ge(exp_ready, GROUPS * j + g + 1)
                        bank = next_bank()
                        for k in range(KG):
                            mm = pe.transpose(bank[0:Q, k * P:(k + 1) * P], prob[:, KG * g + k, :], ident[:, :])
                        mm.then_inc(turn_full[turn_by[n][0]], 1)
                elif kind == "attend":
                    j = step[1]
                    for g in range(GROUPS):
                        wait_turned(pe, turn_of[("pT", j)] + g)
                        for b in (2 * j, 2 * j + 1):
                            wait_ctx(pe, b, g)
                        for k in range(KG * g, KG * g + KG):
                            for h in range(2):
                                mm = pe.matmul(psA[h * TP:(h + 1) * TP, :], probT[0:Q, k, h * TP:(h + 1) * TP],
                                               ctx_sb[0:Q, (2 * j + h) % SLOTS, k, :],
                                               start=(k == 0), stop=(k == KT - 1))
                        mm.then_inc(attended, 1)
                elif kind == "proj":
                    group = step[1]
                    n, N = work_of[step], columns(group)
                    if group[0] == 0:
                        pe.wait_ge(u_in, 16 * 4)
                        pe.wait_ge(v1_in, 16)
                    for p in group:
                        wait_turned(pe, turn_of[("x2T", p)])
                    bank = next_bank()
                    for k in range(KD):
                        mm = pe.matmul(bank[:, 0:N], u1[:, k, :], x2T[:, k, 2 * T * group[0]:2 * T * group[0] + N], start=(k == 0), stop=(k == KD - 1))
                    mm.then_inc(worked, 1)
                elif kind == "ffn":
                    _, group, c = step
                    n, N, f = work_of[step], columns(group), piece(c)
                    if c == 0:
                        pe.wait_ge(pr_ready, FFN_COUNT[group] + 1)
                    bank = next_bank()
                    pe.matmul(bank[0:f, 0:N], v1[:, c * P:c * P + f], prT[:, 0:N], start=True, stop=True)
                    pe.matmul(bank[0:f, 256:256 + N], v1[:, INTER + c * P:INTER + c * P + f], prT[:, 0:N],
                              start=True, stop=True).then_inc(worked, 1)
                    if c >= LAG:
                        inner_sum(group, c - LAG)
                elif kind == "ffn_sum":
                    for c in range(FC - LAG, FC):
                        inner_sum(step[1], c)
                elif kind == "ffn_out":
                    group = step[1]
                    pe.wait_ge(z_ready, FFN_COUNT[group] + 1)
                    for i in range(len(group)):
                        n = work_of[step] + i
                        bank = next_bank()
                        pe.matmul(bank[:, :], zT[:, i].rearrange("p b t -> p (b t)"), v2[:, :],
                                  start=True, stop=True).then_inc(worked, 1)

        @block.vector
        def _(ve):
            chained = [0]

            def link(ins):
                chained[0] += 1
                ins.then_inc(dve_chain, 1)
                ve.wait_ge(dve_chain, chained[0])

            nc.vector.memset(rows[:, :], 0.0).then_inc(rows_zero, 1)
            ve.wait_ge(bv_in, 48)
            link(nc.vector.tensor_scalar(sign, bv, 0.0, 2.0, ALU.is_ge, ALU.mult))
            link(nc.vector.scalar_tensor_tensor(out=bound, in0=sign, scalar=-1.0, in1=bv, op0=ALU.add, op1=ALU.mult,
                                                accum_out=asum[:, :]))
            link(nc.vector.tensor_scalar(bound, sign, -1.0, asum[:, :], ALU.add, ALU.mult))
            link(nc.vector.scalar_tensor_tensor(out=bound, in0=bound, scalar=1.0 / HD, in1=bv,
                                                op0=ALU.mult, op1=ALU.subtract))
            nc.vector.tensor_tensor(bv, bound, bv, ALU.add).then_inc(bound_ready, 1)

            def empty_turns(step, count):
                for i in range(count):
                    n = turn_of[step] + i
                    if turn_by[n][0] == 1:
                        wait_turn_full(ve, n)
                        o, src = turned_into(step, i)
                        nc.vector.tensor_copy(o, src).then_inc(turned[1], 1)

            norms = {}

            def moments(layer, p):
                norms[(layer, p)] = len(norms) + 1
                link(nc.vector.bn_stats(stats[:, layer, p, :], X[:, p, :]))
                nc.vector.bn_aggr(mv[:, layer, p, :], stats[:, layer, p, :]).then_inc(var_ready, 1)

            def normalize(layer, p):
                ve.wait_ge(rstd_ready, norms[(layer, p)])
                return nc.vector.tensor_scalar(X[:, p, :], X[:, p, :], mv[:, layer, p, 0:1], rstd[:, layer, p:p + 1],
                                               ALU.subtract, ALU.mult)

            for step in STEPS:
                kind = step[0]
                if kind == "bind":
                    ve.wait_ge(worked, work_of[step] + 1)
                    link(nc.vector.tensor_copy(bcols[:, :], work(work_of[step])[:, 0:3 * H]))
                    nc.vector.tensor_tensor(qkc[:, :], bcols[:, H:2 * H], bcols[:, 2 * H:3 * H],
                                            ALU.mult).then_inc(qkc_ready, 1)
                elif kind == "columns":
                    ve.wait_ge(worked, work_of[step] + 1)
                    link(nc.vector.tensor_copy(cols[:, :], work(work_of[step])[:, 0:NROW]))
                    nc.vector.tensor_scalar(hcols[:, :], cols[:, 2 * KD:NROW], 0.5, None, ALU.mult).then_inc(cols_ready, 1)
                elif kind in ("wqT", "x1T"):
                    empty_turns(step, 1)
                elif kind == "x2T":
                    if step[1] == 0:
                        ve.wait_ge(v1_in, 16)
                    empty_turns(step, 1)
                elif kind == "ctxT":
                    _, j, g, h = step
                    n = GROUPS * j + g
                    if n >= 2 and h == 0:
                        ve.wait_ge(scored, n - 1)
                    empty_turns(step, KD)
                elif kind == "cross":
                    _, j, g, h = step
                    if h == 0:
                        ve.wait_ge(scored, GROUPS * j + g - 1)
                    loads = BR * (CROSS.index(step) // 2 + 1) + (BR if step == CROSS[-1] else 0)
                    ve.wait_ge(blocks_in[h], 16 * loads)
                    by_piece = blocks[:, h].rearrange("p n (r k) -> p k n r", k=KD)
                    for kd in range(KD):
                        nc.vector.transpose(ctxT[:, (GROUPS * j + g) % 2, h, kd, :].rearrange("p (n r) -> p n r", r=BL),
                                            by_piece[:, kd]).then_inc(crossed, 1)
                elif kind == "pT":
                    if step[1] >= 1:
                        ve.wait_ge(attended, GROUPS * step[1])
                    empty_turns(step, GROUPS)
                elif kind == "self_scores":
                    p, n = step[1], work_of[step]
                    if p == 0:
                        ve.wait_ge(consts, 2)
                    ve.wait_ge(tanh_ready, p + 1)
                    nc.vector.scalar_tensor_tensor(
                        out=selfp[:, p % 2], in0=selfp[:, p % 2], scalar=1.0,
                        in1=mask[:, :].rearrange("p (a t) -> p a t", a=1).to_broadcast([P, H, P]),
                        op0=ALU.add, op1=ALU.mult).then_inc(selfp_ready, 1)
                elif kind == "self_out":
                    p, n = step[1], work_of[step]
                    ve.wait_ge(worked, n + 1)
                    ve.wait_ge(val_ready, p + 1)
                    nc.vector.tensor_tensor(X[:, p, :], work(n), X[:, p, :], ALU.add).then_inc(self_added, 1)
                    ve.wait_ge(self_added, p + 1)
                    moments(0, p)
                elif kind == "norm1":
                    normalize(0, step[1]).then_inc(x1_ready, 1)
                elif kind == "c":
                    p, n = step[1], work_of[step]
                    ve.wait_ge(worked, n + 1)
                    nc.vector.tensor_copy(c_sb[:, p:p + 1], work(n)[:, 0:1]).then_inc(c_ready, 1)
                    if p == PAIRS - 1:
                        ve.wait_ge(c_ready, PAIRS)
                elif kind == "scores":
                    _, j, g = step
                    ve.wait_ge(scored, GROUPS * j + g + 1)
                    last = nc.vector.reduce_max(top[:, g:g + 1], psS[:, g, 0:GC], AX.X)
                    if g == GROUPS - 1:
                        link(last)
                elif kind == "bias":
                    j = step[1]
                    link(nc.vector.reduce_max(topc[:, :], top[:, :], AX.X))
                    link(nc.vector.tensor_tensor(topc[:, :], topc[:, :], c_sb[:, j:j + 1], ALU.add))
                    nc.vector.tensor_scalar(bias[:, :], topc[:, :], c_sb[:, j:j + 1], -X_SCALE,
                                            ALU.subtract, ALU.mult).then_inc(bias_ready, 1)
                elif kind == "attend":
                    j = step[1]
                    ve.wait_ge(exp_ready, GROUPS * (j + 1))
                    link(nc.vector.reduce_sum(dsum[:, :], den[:, :], AX.X))
                    link(nc.vector.reciprocal(rden[:, :], dsum[:, :]))
                    ve.wait_ge(attended, GROUPS * (j + 1))
                    nc.vector.scalar_tensor_tensor(out=X[:, j, :], in0=psA[:, :], scalar=rden[:, :],
                                                   in1=X[:, j, :], op0=ALU.mult, op1=ALU.add).then_inc(att_added, 1)
                    ve.wait_ge(att_added, j + 1)
                    moments(1, j)
                elif kind == "norm2":
                    normalize(1, step[1]).then_inc(x2_ready, 1)
                elif kind == "ffn":
                    _, group, c = step
                    n, N, f = work_of[step], columns(group), piece(c)
                    i = FFN_COUNT[group] * FC + c
                    ve.wait_ge(gate_ready, i + 1)
                    link(nc.vector.scalar_tensor_tensor(out=tanh[0:f, i % 2, 0:N], in0=tanh[0:f, i % 2, 0:N],
                                                        scalar=1.0, in1=gate[0:f, i % 2, 0:N],
                                                        op0=ALU.add, op1=ALU.mult))
                    if c == 0 and FFN_COUNT[group] >= 1:
                        ve.wait_ge(summed, FFN_COUNT[group])
                    nc.vector.scalar_tensor_tensor(out=act[0:f, c, 0:N], in0=work(n)[0:f, 256:256 + N],
                                                   scalar=cols[0:f, 2 * KD + FC + c:2 * KD + FC + c + 1],
                                                   in1=tanh[0:f, i % 2, 0:N],
                                                   op0=ALU.add, op1=ALU.mult).then_inc(act_ready, 1)
                elif kind == "ffn_out":
                    for i, p in enumerate(step[1]):
                        n = work_of[step] + i
                        ve.wait_ge(worked, n + 1)
                        ve.wait_ge(x2b_ready, p + 1)
                        nc.vector.tensor_tensor(X[:, p, :], work(n), X[:, p, :], ALU.add).then_inc(y_added, 1)
                        ve.wait_ge(y_added, p + 1)
                        moments(2, p)
                elif kind == "norm3":
                    normalize(2, step[1]).then_inc(y_ready, 1)


_INS = ['x', 'ctx_4096', 'L0_attn_bv_q', 'L0_attn_bv_k', 'L0_attn_bv_v', 'L0_xattn_Wq', 'L0_xattn_bq', 'L0_xattn_Wk',
        'L0_xattn_bk', 'L0_ffn_U1', 'L0_ffn_V1', 'L0_ffn_U2', 'L0_ffn_V2', 'L0_ffn_b1', 'L0_ffn_b2']


def kernel(**inputs):
    import numpy as _np
    import concourse.bacc as _bacc
    from concourse import mybir as _mybir
    from concourse.bass_utils import run_bass_kernel_spmd as _run

    nc = _bacc.Bacc("TRN2", target_bir_lowering=False, num_devices=1)
    arrays, args = {}, []
    for name in _INS:
        a = _np.ascontiguousarray(inputs[name])
        arrays[f"in_{name}_dram"] = a
        args.append(nc.dram_tensor(f"in_{name}_dram", a.shape, _mybir.dt.from_np(a.dtype), kind="ExternalInput").ap())
    shape = inputs['x'].shape
    out = nc.dram_tensor("out_dram", shape, _mybir.dt.from_np(_np.dtype('float32')), kind="ExternalOutput").ap()
    decoder_layer(nc, *args, out)
    r = _run(nc, [arrays], core_ids=[0])
    return r.results[0]["out_dram"]
```

```python
from contextlib import ExitStack

import concourse.bass as bass
from concourse import mybir

F32 = mybir.dt.float32
F32R = mybir.dt.float32r
ALU = mybir.AluOpType
ACT = mybir.ActivationFunctionType
AX = mybir.AxisListType

P = 128
EPS = 1e-5


FFN_FIRST, FFN_LAST = (0, 1, 2), (3,)
FFN_EARLY = 7
WARM = 5
LAG = 3


def steps(pairs, groups, chunks):
    last = groups - 1
    out = [("xT", 0), ("xT", 1), ("bind",), ("self_scores", 0), ("xT", 2), ("self_scores", 1), ("self_out", 0),
           ("xT", 3), ("self_scores", 2), ("self_out", 1), ("norm1", 0), ("self_scores", 3), ("wqT", 0),
           ("self_out", 2), ("norm1", 1), ("x1T", 0), ("wqT", 1), ("self_out", 3), ("norm1", 2),
           ("x1T", 1), ("wqT", 2), ("norm1", 3), ("x1T", 2), ("wqT", 3), ("columns",),
           ("x1T", 3)] + [("cross", 0, g, h) for g in range(2) for h in range(2)]
    out += [("q", 0), ("wk_split",)] + [("q", m) for m in range(1, 4)]
    out += [("g", m) for m in range(4)] + [("c_parts",)]
    for j in range(pairs):
        out.append(("scores", j, 0))
        if j == 0:
            out += [("c", p) for p in range(pairs)]
        else:
            out.append(("norm2", j - 1))
        if j + 1 == pairs:
            out += [("split", 0), ("split", 1)]
        out += [("cross", j, last, 0), ("cross", j, last, 1)]
        out.append(("scores", j, 1))
        if j > 0:
            out.append(("x2T", j - 1))
        if j + 1 == pairs:
            out.append(("proj", FFN_FIRST))
        out += [("scores", j, last), ("bias", j)]
        if j + 1 < pairs:
            halves = [("ctxT", j + 1, 0, h) for h in range(2)]
        else:
            halves = [("ffn", FFN_FIRST, c) for c in range(FFN_EARLY)]
        for g in range(groups):
            out += halves[g:g + 1] + [("exp", j, g)]
        out += halves[groups:] + [("pT", j)]
        if j + 1 < pairs:
            out += [("cross", j + 1, 1, 0), ("cross", j + 1, 1, 1)]
        out.append(("attend", j))
    out += [("ffn", FFN_FIRST, c) for c in range(FFN_EARLY, chunks - 2)] + [("norm2", pairs - 1)]
    out += [("ffn", FFN_FIRST, chunks - 2), ("x2T", pairs - 1), ("ffn", FFN_FIRST, chunks - 1)]
    out += [("proj", FFN_LAST), ("ffn_sum", FFN_FIRST)]
    out += [("ffn", FFN_LAST, c) for c in range(chunks)]
    out += [("ffn_out", 0), ("ffn_sum", FFN_LAST), ("norm3", 0), ("ffn_out", 1), ("norm3", 1), ("ffn_out", 3),
            ("norm3", 3), ("ffn_out", 2), ("norm3", 2)]
    return out


def decoder_layer(nc, x, ctx, bv_q, bv_k, bv_v, Wq, bq, Wk, bk, U1, V1, U2, V2, b1, b2, out):
    B, T, D = x.shape
    S = ctx.shape[1]
    H, HD = bv_q.shape
    R = U1.shape[1]
    INTER = U2.shape[0]
    PAIRS = B // 2
    TP = P // 2
    KD = D // P
    KT = 12
    Q = S // KT
    GROUPS = 3
    KG = KT // GROUPS
    GC = KG * Q
    BL = 32
    NB = -(-GC // BL)
    BR = P // BL
    FC = -(-INTER // P)
    FT = INTER - (FC - 1) * P
    RING = 5
    SLOTS = 4
    SELF_SCALE = 4.0 * float(HD) ** -0.5
    X_SCALE = float(D) ** -0.5
    SPLIT = 4
    HALF = 256
    GB = 4
    QA = 112
    assert D == 512 and HD == P and H == KD and R == P and Q * KT == S and Q <= P and GC <= 512
    assert PAIRS == 4 and T <= TP

    STEPS = steps(PAIRS, GROUPS, FC)

    es = ExitStack()
    with es:
        def sb(name, shape):
            return es.enter_context(nc.sbuf_tensor(name, shape, F32))

        def ps(name, shape):
            return es.enter_context(nc.psum_tensor(name, shape, F32))

        def sem(name):
            return es.enter_context(nc.semaphore(name))

        ctx_at = -(-nc.sbuf_base // 32) * 32
        ctx_sb = sb("ctx_sb", [P, SLOTS, KT, D])
        ctxT = sb("ctxT", [P, 2, 2, KD, NB * BL])
        prob = sb("prob", [P, KT, Q])
        probT = sb("probT", [P, KT, P])
        zeros = ctxT[:, 0, 0, 0, :]
        X = sb("X", [P, PAIRS, D])
        gT_tiles = sb("gT_tiles", [P, KD, B - 2, TP])
        gT = sb("gT", [P, KD, B, TP])
        b2_rows = sb("b2_rows", [P, D])
        shared = sb("shared", [P, 8192 + KD * B * T])
        wkv = shared[:, 0:2048].rearrange("p (k x) -> p k x", k=KD)
        wqT = shared[:, 2048:4096].rearrange("p (k x) -> p k x", k=KD)
        qT = shared[:, 4096:6144].rearrange("p (k b t) -> p k b t", k=KD, b=B)
        x1T = shared[:, 6144:6144 + KD * B * T].rearrange("p (k b t) -> p k b t", k=KD, b=B)
        NMAX = 2 * T * len(FFN_FIRST)
        v1 = shared[:, 0:2 * INTER]
        at = 2 * INTER
        x2T = shared[:, at:at + KD * B * T].rearrange("p (k n) -> p k n", k=KD)
        at += KD * B * T
        u1 = shared[:, at:at + KD * R].rearrange("p (k r) -> p k r", k=KD)
        at += KD * R
        v2 = shared[:, at:at + D]
        at += D
        blocks = shared[:, at:at + 2 * NB * P].rearrange("p (a n x) -> p a n x", a=2, n=NB)
        assert at + 2 * NB * P <= 8192 + KD * B * T
        prT = shared[:, at:at + NMAX]
        at += NMAX
        gate = shared[:, at:at + GB * NMAX].rearrange("p (a n) -> p a n", a=GB)
        at += GB * NMAX
        tanh = shared[:, at:at + GB * NMAX].rearrange("p (a n) -> p a n", a=GB)
        at += GB * NMAX
        assert at <= 8192 + KD * B * T
        zT = sb("zT", [P, PAIRS, 2, TP])
        act = ctx_sb[:, 0].rearrange("p k x -> p (k x)")[:, 0:FC * NMAX].rearrange("p (c n) -> p c n", c=FC)
        late = ctx_sb[:, 0:2].rearrange("p a k x -> p (a k x)")
        at = FC * NMAX
        u2 = late[:, at:at + FC * R].rearrange("p (c r) -> p c r", c=FC)
        at += FC * R
        assert at + 4 * INTER + 2 * NMAX <= 2 * KT * D

        def in_slot(name, slot, g, words):
            at = ctx_at + 4 * D * (KT * slot + KG * g)
            return nc.alloc_sbuf_tensor_at(name, [P, words], F32R, offset=at)

        wk_high = in_slot("wk_high", 3, 1, KD * D)[:, :].rearrange("p (k x) -> p k x", k=KD)
        wk_low = in_slot("wk_low", 3, 2, KD * D)[:, :].rearrange("p (k x) -> p k x", k=KD)
        q_high = in_slot("q_high", 0, 2, KD * B * T)[:, :].rearrange("p (k n) -> p k n", k=KD)
        q_low = in_slot("q_low", 1, 2, KD * B * T)[:, :].rearrange("p (k n) -> p k n", k=KD)
        late_split = nc.alloc_sbuf_tensor_at("late_split", [P, 4 * INTER + 2 * NMAX], F32R, offset=ctx_at + 4 * at)
        v1_high = late_split[:, 0:2 * INTER]
        v1_low = late_split[:, 2 * INTER:4 * INTER]
        pr_high = late_split[:, 4 * INTER:4 * INTER + NMAX]
        pr_low = late_split[:, 4 * INTER + NMAX:4 * INTER + 2 * NMAX]
        early = ctx_sb[:, SLOTS - 1].rearrange("p k x -> p (k x)")
        wq = early[:, 0:2048].rearrange("p (k x) -> p k x", k=KD)
        xT = early[:, 2048:3072].rearrange("p (a h t) -> p a h t", a=2, h=H)
        kqT = early[:, 3072:4096].rearrange("p (a h t) -> p a h t", a=2, h=H)
        selfp = early[:, 4096:5120].rearrange("p (a h t) -> p a h t", a=2, h=H)
        val = early[:, 5120:6144].rearrange("p (a n) -> p a n", a=2)

        ident = sb("ident", [P, P])
        mask = sb("mask", [P, P])
        NROW = 2 * KD + 2 * FC
        start = prob[:, :, :].rearrange("p k q -> p (k q)")
        vdiag = start[0:H, 0:D].rearrange("p (h d) -> p h d", h=H)
        ones = start[0:H, D + 3 * P:D + 4 * P]
        rows = start[0:NROW, D + 4 * P:D + 5 * P]
        bv = probT[0:3 * H, H, :]
        sign = probT[0:3 * H, H + 1, :]
        bound = probT[0:3 * H, H + 2, :]
        v_rows = probT[:, 0:H, :].rearrange("p h d -> p (h d)")
        cols = sb("cols", [P, 2 * KD + 2 * FC])
        hcols = sb("hcols", [P, 2 * FC])
        asum = sb("asum", [3 * H, 1])
        bcols = sb("bcols", [P, 3 * H])
        qkc = sb("qkc", [P, H])
        c_sb = sb("c_sb", [P, PAIRS])
        bk_columns = probT[:, 2 * H, :].rearrange("p (k a) -> p k a", k=KD)
        c_parts = start[:, 0:B * TP]
        top = sb("top", [P, GROUPS])
        topc = sb("topc", [P, 1])
        bias = sb("bias", [P, 1])
        den = sb("den", [P, GROUPS])
        dsum = sb("dsum", [P, 1])
        rden = sb("rden", [P, 1])
        stats = sb("stats", [P, 3, PAIRS, 6])
        mv = sb("mv", [P, 3, PAIRS, 2])
        veps = sb("veps", [P, 3, PAIRS])
        rstd = sb("rstd", [P, 3, PAIRS])
        shift = sb("shift", [P, 3, PAIRS])
        mhalf = sb("mhalf", [P, 1])

        psS = ps("psS", [P, GROUPS, 512])
        ring = ps("ring", [P, RING, 512])
        psA = psS[:, GROUPS - 1]
        psZ = psS[:, 0]

        x_in = [sem("x_in01"), sem("x_in2"), sem("x_in3")]
        bv_in, rows_in, b2_in = sem("bv_in"), sem("rows_in"), sem("b2_in")
        wq_in, wk_in = sem("wq_in"), sem("wk_in")
        u1_in, v1_in, u2_in, v2_in = sem("u1_in"), sem("v1_in"), sem("u2_in"), sem("v2_in")
        ctx_in = [[sem(f"ctx_in{s}_{g}") for g in range(GROUPS)] for s in range(SLOTS)]
        zeros_ready = sem("zeros_ready")
        rows_zero = sem("rows_zero")
        consts = sem("consts")
        pool_chain = sem("pool_chain")
        dve_chain = sem("dve_chain")
        bound_ready = sem("bound_ready")
        qkc_ready = sem("qkc_ready")
        vdiag_ready = sem("vdiag_ready")
        cols_ready = sem("cols_ready")
        v_rows_ready = sem("v_rows_ready")
        kq_ready = sem("kq_ready")
        val_ready = sem("val_ready")
        tanh_ready = sem("tanh_ready")
        selfp_ready = sem("selfp_ready")
        var_ready = sem("var_ready")
        rstd_ready = sem("rstd_ready")
        x1_ready = sem("x1_ready")
        x2_ready = sem("x2_ready")
        x2b_ready = sem("x2b_ready")
        q_ready = sem("q_ready")
        c_ready = sem("c_ready")
        c_parts_ready = sem("c_parts_ready")
        q_high_ready, q_low_ready = sem("q_high_ready"), sem("q_low_ready")
        wk_high_ready, wk_low_ready = sem("wk_high_ready"), sem("wk_low_ready")
        g_tiles_ready = sem("g_tiles_ready")
        g_ready, g_dve_ready = sem("g_ready"), sem("g_dve_ready")
        blocks_in = [sem("blocks_in0"), sem("blocks_in1")]
        first_blocks_in = [[sem(f"first_blocks_in{g}_{h}") for h in range(2)] for g in range(GROUPS)]
        crossed = sem("crossed")
        scored = sem("scored")
        bias_ready = sem("bias_ready")
        exp_ready = sem("exp_ready")
        attended = sem("attended")
        turn_full = [sem("turn_full_act"), sem("turn_full_dve")]
        turned = [sem("turned_act"), sem("turned_dve")]
        worked = sem("worked")
        v_bound = sem("v_bound")
        summed = sem("summed")
        self_added = sem("self_added")
        att_added = sem("att_added")
        y_added = sem("y_added")
        pr_ready = sem("pr_ready")
        pr_low_ready = sem("pr_low_ready")
        v1_high_ready = sem("v1_high_ready")
        v1_low_ready = sem("v1_low_ready")
        gate_ready = sem("gate_ready")
        act_ready = sem("act_ready")
        z_ready = sem("z_ready")
        y_ready = sem("y_ready")
        out_sem = sem("out_sem")

        FFN_COUNT = {g: i for i, g in enumerate((FFN_FIRST, FFN_LAST))}

        OUTS = [s[1] for s in STEPS if s[0] == "ffn_out"]
        STORES = [s[1] for s in STEPS if s[0] == "norm3"]
        NORMS = [({"self_out": 0, "attend": 1, "ffn_out": 2}[s[0]], s[1]) for s in STEPS
                 if s[0] in ("self_out", "attend", "ffn_out")]

        def by_act(layer, p):
            return layer == 0 or (layer == 2 and p != STORES[-1])

        def banks_of(group):
            return 1 if len(group) * 2 * T <= HALF else 2

        turn_of, work_of = {}, {}
        turn_bank, work_bank = [], []
        turn_by = []
        by_engine = [0, 0]
        job_read = []
        for s in STEPS:
            kind = s[0]
            turns = {"xT": 1, "wqT": 1, "x1T": 1, "x2T": 1, "ctxT": KD, "pT": GROUPS}.get(kind, 0)
            if turns:
                turn_of[s] = len(turn_bank)
                for i in range(turns):
                    e = int(kind == "ctxT" and KD * s[3] + i >= 3)
                    by_engine[e] += 1
                    turn_by.append((e, by_engine[e]))
                    turn_bank.append(len(job_read) % RING)
                    job_read.append((kq_ready, H * (s[1] + 1)) if kind == "xT" else (turned[e], by_engine[e]))
            read = {"bind": qkc_ready, "columns": cols_ready, "self_scores": tanh_ready, "self_out": self_added,
                    "q": q_high_ready, "g": g_tiles_ready, "c_parts": c_parts_ready, "c": c_ready,
                    "proj": pr_ready, "ffn": act_ready, "ffn_out": y_added}.get(kind)
            if read is not None:
                work_of[s] = len(work_bank)
                if kind == "proj":
                    done = [FFN_COUNT[s[1]] + 1]
                    if s[1] == FFN_FIRST:
                        read = pr_low_ready
                elif kind == "ffn":
                    done = [FFN_COUNT[s[1]] * FC + s[2] + 1] * banks_of(s[1])
                elif kind == "ffn_out":
                    done = [OUTS.index(s[1]) + 1]
                elif kind in ("bind", "columns", "c_parts"):
                    done = [1]
                else:
                    done = [s[1] + 1]
                for i, d in enumerate(done):
                    work_bank.append(len(job_read) % RING)
                    job_read.append((gate_ready if kind == "ffn" and i + 1 < len(done) else read, d))

        def gated(group, n):
            return work(n)[:, HALF:] if banks_of(group) == 1 else work(n + 1)

        def turn(n):
            return ring[:, turn_bank[n]]

        def work(n):
            return ring[:, work_bank[n]]

        def wait_turned(eng, first, count=1):
            for e in range(2):
                counts = [c for by, c in turn_by[first:first + count] if by == e]
                if counts:
                    eng.wait_ge(turned[e], counts[-1])

        def wait_turn_full(eng, n):
            e, count = turn_by[n]
            eng.wait_ge(turn_full[e], count)

        def turned_into(step, i):
            n = turn_of[step] + i
            bank = turn(n)
            kind = step[0]
            if kind == "xT":
                return xT[:, step[1] % 2], bank.rearrange("p (h t) -> p h t", h=H)
            if kind == "wqT":
                m = step[1]
                return wqT[:, :, m * P:(m + 1) * P], bank.rearrange("p (k t) -> p k t", k=KD)
            if kind in ("x1T", "x2T"):
                src = bank.rearrange("p (k b t) -> p k b t", k=KD, b=2)[:, :, :, 0:T]
                p = step[1]
                if kind == "x1T":
                    return x1T[:, :, 2 * p:2 * p + 2, :], src
                return x2T[:, :, 2 * T * p:2 * T * (p + 1)].rearrange("p k (b t) -> p k b t", b=2), src
            if kind == "ctxT":
                _, j, g, h = step
                return ctxT[:, (GROUPS * j + g) % 2, h, i, 0:GC], bank[:, 0:GC]
            return probT[0:Q, KG * i:KG * i + KG, :], bank[0:Q].rearrange("p (k t) -> p k t", k=KG)

        def split_columns(part, v):
            a, b = (0, SPLIT * P) if part == 0 else (SPLIT * P, INTER)
            return v.rearrange("p (h n) -> p h n", h=2)[:, :, a:b]

        def columns(group):
            return len(group) * 2 * T

        def wait_x(eng, p):
            if p < 2:
                eng.wait_ge(x_in[0], 32)
            else:
                eng.wait_ge(x_in[1], 32)
            if p == 3:
                eng.wait_ge(x_in[2], 32)

        def wait_ctx(eng, b, g):
            eng.wait_ge(ctx_in[b % SLOTS][g], 32 * (b // SLOTS + 1))

        CROSS = [s for s in STEPS if s[0] == "cross"]
        FIRST = [s for s in CROSS if s[1] == 0]

        def block_buffer(step):
            _, j, g, h = step
            if j == 0:
                slot, at = (h, g) if g < GROUPS - 1 else (2, 1 + h)
                buffer = ctx_sb[:, slot, KG * at:KG * at + KG, :].rearrange("p k (n x) -> p (k n) x", x=P)
                return buffer, first_blocks_in[g][h], BR
            done = (CROSS.index(step) - len(FIRST)) // 2 + 1
            return blocks[:, h], blocks_in[h], BR * (done + (step == CROSS[-1]))

        def piece(c):
            return P if c < FC - 1 else FT

        block = es.enter_context(nc.Block())

        @block.sync
        def _(sp):
            def load_x(h, p0, count, rows_):
                src = bass.AP(tensor=x.tensor, offset=(2 * p0 + h) * T * D,
                              ap=[[D, rows_], [2 * T * D, count], [1, D]])
                sp.dma_start(X[h * TP:h * TP + rows_, p0:p0 + count, :], src).then_inc(x_in[p0 // 2 + p0 // 3], 16)

            load_x(0, 0, 2, TP)
            load_x(1, 0, 2, TP)
            load_x(0, 2, 2, TP)
            load_x(1, 2, 1, TP)
            load_x(1, 3, 1, T)
            sp.dma_start(X[TP + T:P, PAIRS - 1, :], x[0, 0:TP - T, :]).then_inc(x_in[2], 16)

            def load_ctx(b, g):
                slot = b % SLOTS
                if b >= SLOTS:
                    sp.wait_ge(attended, GROUPS * (b // 2 - SLOTS // 2) + g + 1)
                v = ctx[b, GC * g:GC * g + GC].rearrange("(k q) x -> q k x", k=KG)
                ks = slice(KG * g, KG * g + KG)
                for q0, q1 in ((0, QA), (QA, Q)):
                    sp.dma_start(ctx_sb[q0:q1, slot, ks, :], v[q0:q1]).then_inc(ctx_in[slot][g], 16)

            def load_blocks(step):
                _, j, g, h = step
                buffer, loaded, _ = block_buffer(step)
                i = CROSS.index(step)
                if i >= len(FIRST) + 2:
                    sp.wait_ge(crossed, KD * (i - 1))
                row = (2 * j + h) * S + GC * g
                full = NB if step != CROSS[-1] else NB - 1
                for r in (0, 2, 1, 3):
                    src = bass.AP(tensor=ctx.tensor, offset=row * D + P * r, ap=[[D, BL], [BL * D, full], [1, P]])
                    sp.dma_start(buffer[BL * r:BL * r + BL, 0:full, :], src).then_inc(loaded, 16)
                if full < NB:
                    left = GC - full * BL
                    src = ctx[2 * j + h, S - left:S].rearrange("r (i x) -> i r x", x=P)
                    for r in range(BR):
                        sp.dma_start(buffer[BL * r:BL * r + left, full, :], src[r]).then_inc(loaded, 16)

            sp.dma_start(wq, Wq.rearrange("(k p) x -> p k x", p=P)).then_inc(wq_in, 16)
            sp.wait_ge(rows_zero, 1)
            sp.dma_start(rows[0:KD, :], bq.rearrange("(k p) -> k p", p=P)).then_inc(rows_in, 16)
            sp.dma_start(rows[KD:2 * KD, :], bk.rearrange("(k p) -> k p", p=P)).then_inc(rows_in, 16)
            for h in range(2):
                r, o = 2 * KD + h * FC, h * INTER
                sp.dma_start(rows[r:r + FC - 1, :], b1[o:o + (FC - 1) * P].rearrange("(k p) -> k p", p=P))\
                  .then_inc(rows_in, 16)
                sp.dma_start(rows[r + FC - 1:r + FC, 0:FT],
                             b1[o + (FC - 1) * P:o + INTER].rearrange("(a p) -> a p", a=1)).then_inc(rows_in, 16)
            for step in FIRST:
                load_blocks(step)
            sp.dma_start(wkv, Wk.rearrange("(k p) x -> p k x", p=P)).then_inc(wk_in, 16)
            sp.dma_start(b2_rows[:, :], b2.rearrange("(a n) -> a n", a=1).to_broadcast([P, D])).then_inc(b2_in, 16)
            load_ctx(2, 0)
            n = work_of[("self_out", PAIRS - 1)]
            sp.wait_ge(worked, n + 1)
            n = turn_of[("wqT", KD - 1)]
            wait_turn_full(sp, n)
            load_ctx(3, 0)
            for g in range(GROUPS - 1):
                for h in range(2):
                    sp.wait_ge(crossed, KD * (CROSS.index(("cross", 0, g, h)) + 1))
                    load_ctx(h, g)
            sp.wait_ge(wk_low_ready, 1)
            n = work_of[("q", KD - 1)]
            sp.wait_ge(worked, n + 1)
            sp.dma_start(v1, V1).then_inc(v1_in, 16)
            n = work_of[("g", KD - 1)]
            sp.wait_ge(worked, n + 1)
            load_ctx(0, GROUPS - 1)
            load_ctx(1, GROUPS - 1)
            n = work_of[("c_parts",)]
            sp.wait_ge(worked, n + 1)
            later = iter(CROSS[len(FIRST):])
            load_blocks(next(later))
            load_blocks(next(later))
            load_ctx(3, 1)
            load_ctx(3, 2)
            sp.dma_start(u1, U1.rearrange("(k p) r -> p k r", p=P)).then_inc(u1_in, 16)
            sp.dma_start(v2, V2).then_inc(v2_in, 16)
            for h in range(2):
                sp.wait_ge(crossed, KD * (CROSS.index(("cross", 0, GROUPS - 1, h)) + 1))
                load_ctx(2, 1 + h)
            load_blocks(next(later))
            load_blocks(next(later))
            for j in range(SLOTS // 2, PAIRS):
                for g in range(GROUPS - 1):
                    load_ctx(2 * j, g)
                    load_ctx(2 * j + 1, g)
                load_blocks(next(later))
                load_blocks(next(later))
                load_ctx(2 * j, GROUPS - 1)
                load_ctx(2 * j + 1, GROUPS - 1)
                load_blocks(next(later))
                load_blocks(next(later))
            sp.wait_ge(attended, GROUPS * (PAIRS - 1))
            sp.dma_start(u2[:, 0:FC - 1, :], U2[0:(FC - 1) * P].rearrange("(c p) r -> p c r", p=P)).then_inc(u2_in, 16)
            sp.dma_start(u2[0:FT, FC - 1, :], U2[(FC - 1) * P:INTER]).then_inc(u2_in, 16)
            for i, p in enumerate(STORES):
                sp.wait_ge(y_ready, i + 1)
                for h in range(2):
                    sp.dma_start(out[2 * p + h], X[h * TP:h * TP + T, p, :]).then_inc(out_sem, 16)
            sp.wait_ge(out_sem, 16 * B)

        @block.gpsimd
        def _(pool):
            chained = [0]

            def link(ins):
                chained[0] += 1
                ins.then_inc(pool_chain, 1)
                pool.wait_ge(pool_chain, chained[0])

            for i, src in enumerate((bv_v, bv_q, bv_k)):
                pool.dma_start(bv[i * H:(i + 1) * H, :], src).then_inc(bv_in, 16)
            link(nc.gpsimd.memset(ident[:, :], 0.0))
            nc.gpsimd.affine_select(out=ident[:, :], in_=ident[:, :], compare_op=ALU.not_equal, fill=1.0,
                                    base=0, pattern=[[-1, P]], channel_multiplier=1).then_inc(consts, 1)
            nc.gpsimd.memset(ones[:, :], 1.0)
            nc.gpsimd.memset(mhalf[:, :], -0.5)
            link(nc.gpsimd.memset(mask[:, :], 0.5))
            link(nc.gpsimd.affine_select(out=mask[:, :], in_=mask[:, :], compare_op=ALU.is_ge, fill=0.0,
                                         base=0, pattern=[[1, P]], channel_multiplier=-1))
            nc.gpsimd.memset(mask[0:TP, TP:P], 0.0).then_inc(consts, 1)
            pool.wait_ge(bound_ready, 1)
            nc.gpsimd.affine_select(out=vdiag[:, :, :], in_=probT[0:H, H:H + 1, :].to_broadcast([H, H, P]),
                                    compare_op=ALU.is_equal, fill=0.0, base=0,
                                    pattern=[[-1, H], [0, P]], channel_multiplier=1).then_inc(vdiag_ready, 1)
            nc.gpsimd.memset(qT[:, :, :, T:TP], 0.0)
            nc.gpsimd.memset(gT[:, :, :, T:TP], 0.0)
            nc.gpsimd.memset(gT_tiles[:, :, :, T:TP], 0.0)
            nc.gpsimd.memset(zT[:, :, :, T:TP], 0.0).then_inc(consts, 1)
            pool.wait_ge(v_rows_ready, 1)
            def inverse_deviation(layer, p):
                pool.wait_ge(var_ready, NORMS.index((layer, p)) + 1)
                link(nc.gpsimd.tensor_scalar(veps[:, layer, p:p + 1], mv[:, layer, p, 1:2], EPS, None, ALU.add))
                last = nc.gpsimd.tensor_tensor(rstd[:, layer, p:p + 1], veps[:, layer, p:p + 1], mhalf[:, :], ALU.pow)
                if by_act(layer, p):
                    link(last)
                    last = nc.gpsimd.tensor_scalar(shift[:, layer, p:p + 1], mv[:, layer, p, 0:1],
                                                   rstd[:, layer, p:p + 1], -1.0, ALU.mult, ALU.mult)
                last.then_inc(rstd_ready, 1)

            for step in STEPS:
                kind = step[0]
                if kind == "xT":
                    p = step[1]
                    wait_x(pool, p)
                    if p >= 2:
                        n = work_of[("self_out", p - 2)]
                        pool.wait_ge(worked, n + 1)
                    nc.gpsimd.tensor_tensor(val[:, p % 2, :], X[:, p, :], v_rows[:, :],
                                            ALU.mult).then_inc(val_ready, 1)
                elif kind == "self_out":
                    inverse_deviation(0, step[1])
                elif kind == "attend":
                    inverse_deviation(1, step[1])
                elif kind == "ffn_out":
                    inverse_deviation(2, step[1])
                elif kind == "x2T":
                    p = step[1]
                    n = turn_of[step]
                    pool.wait_ge(b2_in, 16)
                    wait_turn_full(pool, n)
                    nc.gpsimd.tensor_tensor(X[:, p, :], X[:, p, :], b2_rows[:, :], ALU.add).then_inc(x2b_ready, 1)

        @block.scalar
        def _(sc):
            nc.scalar.preload_act_table(ACT.Tanh)

            def normalize(layer, p):
                sc.wait_ge(rstd_ready, NORMS.index((layer, p)) + 1)
                return nc.scalar.activation(X[:, p, :], X[:, p, :], ACT.Identity, bias=shift[:, layer, p:p + 1],
                                            scale=rstd[:, layer, p:p + 1])

            def empty_turns(step, count):
                for i in range(count):
                    n = turn_of[step] + i
                    if turn_by[n][0] == 0:
                        wait_turn_full(sc, n)
                        o, src = turned_into(step, i)
                        nc.scalar.activation(o, src, ACT.Copy).then_inc(turned[0], 1)

            for step in STEPS:
                kind = step[0]
                if kind == "xT":
                    p = step[1]
                    if p >= 2:
                        n = work_of[("self_scores", p - 2)]
                        sc.wait_ge(worked, n + 1)
                    empty_turns(step, 1)
                    if p == 0:
                        sc.wait_ge(qkc_ready, 1)
                    for h in range(H):
                        nc.scalar.activation(kqT[:, p % 2, h, :], turn(turn_of[step])[:, h * P:(h + 1) * P],
                                             ACT.Copy, scale=qkc[:, h:h + 1]).then_inc(kq_ready, 1)
                elif kind == "bind":
                    sc.wait_ge(v_bound, 1)
                    nc.scalar.activation(v_rows[:, :], psA[:, :], ACT.Copy).then_inc(v_rows_ready, 1)
                elif kind in ("wqT", "x1T"):
                    empty_turns(step, 1)
                elif kind == "x2T":
                    if step[1] == 0:
                        sc.wait_ge(worked, work_of[("c_parts",)] + 1)
                    empty_turns(step, 1)
                elif kind == "ctxT":
                    _, j, g, h = step
                    n = GROUPS * j + g
                    if n >= 2 and h == 0:
                        sc.wait_ge(scored, n - 1)
                    empty_turns(step, KD)
                elif kind == "pT":
                    if step[1] >= 1:
                        sc.wait_ge(attended, GROUPS * step[1])
                    empty_turns(step, GROUPS)
                elif kind == "self_scores":
                    p, n = step[1], work_of[step]
                    sc.wait_ge(worked, n + 1)
                    if p >= 2:
                        m = work_of[("self_out", p - 2)]
                        sc.wait_ge(worked, m + 1)
                    nc.scalar.activation(selfp[:, p % 2], work(n).rearrange("p (h t) -> p h t", h=H),
                                         ACT.Tanh, scale=0.5 * SELF_SCALE).then_inc(tanh_ready, 1)
                elif kind == "q":
                    m, n = step[1], work_of[step]
                    sc.wait_ge(worked, n + 1)
                    if m == 0:
                        sc.wait_ge(consts, 3)
                        sc.wait_ge(cols_ready, 1)
                    nc.scalar.activation(qT[:, m, :, 0:T],
                                         work(n)[:, 0:B * T].rearrange("p (b t) -> p b t", b=B),
                                         ACT.Identity, bias=cols[:, m:m + 1]).then_inc(q_ready, 1)
                    nc.scalar.activation(q_high[:, m], work(n)[:, 0:B * T], ACT.Identity,
                                         bias=cols[:, m:m + 1]).then_inc(q_high_ready, 1)
                elif kind == "c_parts":
                    sc.wait_ge(worked, work_of[step] + 1)
                    nc.scalar.activation(c_parts, work(work_of[step]), ACT.Copy).then_inc(c_parts_ready, 1)
                elif kind == "wk_split":
                    sc.wait_ge(wk_in, 16)
                    nc.scalar.activation(wk_high, wkv, ACT.Copy).then_inc(wk_high_ready, 1)
                elif kind == "g":
                    m, n = step[1], work_of[step]
                    sc.wait_ge(worked, n + 1)
                    for k in (0, 1):
                        nc.scalar.activation(gT[BL * m:BL * m + BL, k, :, 0:T],
                                             work(n)[BL * k:BL * k + BL, 0:B * T].rearrange("p (b t) -> p b t", b=B),
                                             ACT.Copy).then_inc(g_ready, 1)
                elif kind == "exp":
                    _, j, g = step
                    if g == 0:
                        sc.wait_ge(bias_ready, j + 1)
                    if g == 0 and j >= 1:
                        wait_turn_full(sc, turn_of[("pT", j - 1)] + GROUPS - 1)
                        wait_turn_full(sc, turn_of[("pT", j - 1)] + GROUPS - 2)
                    nc.scalar.activation(prob[:, KG * g:KG * g + KG, :],
                                         psS[:, g, 0:GC].rearrange("p (k q) -> p k q", k=KG),
                                         ACT.Exp, bias=bias[:, :], scale=X_SCALE,
                                         accum_out=den[:, g:g + 1]).then_inc(exp_ready, 1)
                elif kind == "proj":
                    n, N = work_of[step], columns(step[1])
                    sc.wait_ge(worked, n + 1)
                    nc.scalar.activation(pr_high if step[1] == FFN_FIRST else prT[:, 0:N], work(n)[:, 0:N],
                                         ACT.Copy).then_inc(pr_ready, 1)
                elif kind == "split":
                    if step[1] == 0:
                        sc.wait_ge(v1_in, 16)
                        sc.wait_ge(attended, GROUPS * (PAIRS - 1))
                    nc.scalar.activation(split_columns(step[1], v1_high), split_columns(step[1], v1),
                                         ACT.Copy).then_inc(v1_high_ready, 1)
                elif kind == "ffn":
                    _, group, c = step
                    n, N, f = work_of[step], columns(group), piece(step[2])
                    i = FFN_COUNT[group] * FC + c
                    sc.wait_ge(worked, n + 1)
                    if i == 0:
                        sc.wait_ge(crossed, KD * len(CROSS))
                    if i >= GB:
                        sc.wait_ge(act_ready, i - GB + 1)
                    nc.scalar.activation(tanh[0:f, i % GB, 0:N], work(n)[0:f, 0:N], ACT.Tanh,
                                         bias=hcols[0:f, c:c + 1], scale=0.5)
                    nc.scalar.activation(gate[0:f, i % GB, 0:N], work(n)[0:f, 0:N], ACT.Identity,
                                         bias=cols[0:f, 2 * KD + c:2 * KD + c + 1]).then_inc(gate_ready, 1)
                elif kind == "ffn_sum":
                    group = step[1]
                    sc.wait_ge(summed, FFN_COUNT[group] + 1)
                    nc.scalar.activation(zT[:, group[0]:group[-1] + 1, :, 0:T],
                                         psZ[:, 0:columns(group)].rearrange("p (a b t) -> p a b t", b=2, t=T),
                                         ACT.Copy, scale=0.5).then_inc(z_ready, 1)
                elif kind == "norm1":
                    normalize(0, step[1]).then_inc(x1_ready, 1)
                elif kind == "norm3" and by_act(2, step[1]):
                    normalize(2, step[1]).then_inc(y_ready, 1)

        @block.tensor
        def _(pe):
            jobs = [0]

            def next_bank():
                if jobs[0] >= RING:
                    pe.wait_ge(*job_read[jobs[0] - RING])
                jobs[0] += 1
                return ring[:, (jobs[0] - 1) % RING]

            pe.wait_ge(zeros_ready, 1)
            for _ in range(WARM):
                pe.matmul(psS[:, 0, 0:2 * P], zeros[:, 0:P], zeros[:, 0:2 * P], start=True, stop=True)
            pe.wait_ge(consts, 1)

            def inner_sum(group, c):
                i, N, f = FFN_COUNT[group] * FC + c, columns(group), piece(c)
                pe.wait_ge(act_ready, i + 1)
                if c == 0:
                    pe.wait_ge(u2_in, 16 * 2)
                    if FFN_COUNT[group] == 0:
                        pe.wait_ge(exp_ready, GROUPS * (PAIRS - 1) + 1)
                    else:
                        pe.wait_ge(z_ready, FFN_COUNT[group])
                mm = pe.matmul(psZ[:, 0:N], u2[0:f, c, :], act[0:f, c, 0:N], start=(c == 0), stop=(c == FC - 1))
                if c == FC - 1:
                    mm.then_inc(summed, 1)

            for step in STEPS:
                kind = step[0]
                if kind == "xT":
                    p, n = step[1], turn_of[step]
                    wait_x(pe, p)
                    bank = next_bank()
                    for h in range(H):
                        mm = pe.transpose(bank[:, h * P:(h + 1) * P], X[:, p, h * P:(h + 1) * P], ident[:, :])
                    mm.then_inc(turn_full[turn_by[n][0]], 1)
                elif kind == "bind":
                    bank = next_bank()
                    pe.wait_ge(bound_ready, 1)
                    pe.transpose(bank[:, 0:3 * H], bv, ident[0:3 * H, 0:3 * H]).then_inc(worked, 1)
                    pe.wait_ge(vdiag_ready, 1)
                    pe.matmul(psA, ones, vdiag.rearrange("k h d -> k (h d)"),
                              start=True, stop=True).then_inc(v_bound, 1)
                elif kind == "columns":
                    bank = next_bank()
                    pe.wait_ge(rows_in, 16 * 6)
                    pe.transpose(bank[:, 0:NROW], rows, ident[0:NROW, 0:NROW]).then_inc(worked, 1)
                elif kind == "self_scores":
                    p, n = step[1], work_of[step]
                    bank = next_bank()
                    pe.wait_ge(kq_ready, H * (p + 1))
                    for h in range(H):
                        mm = pe.matmul(bank[:, h * P:(h + 1) * P], kqT[:, p % 2, h, :], xT[:, p % 2, h, :],
                                       start=True, stop=True)
                    mm.then_inc(worked, 1)
                elif kind == "self_out":
                    p, n = step[1], work_of[step]
                    bank = next_bank()
                    pe.wait_ge(selfp_ready, p + 1)
                    pe.wait_ge(val_ready, p + 1)
                    for h in range(H):
                        mm = pe.matmul(bank[:, h * P:(h + 1) * P], selfp[:, p % 2, h, :],
                                       val[:, p % 2, h * P:(h + 1) * P], start=True, stop=True)
                    mm.then_inc(worked, 1)
                elif kind == "wqT":
                    m, n = step[1], turn_of[step]
                    if m == 0:
                        pe.wait_ge(wq_in, 16)
                    bank = next_bank()
                    for k in range(KD):
                        mm = pe.transpose(bank[:, k * P:(k + 1) * P], wq[:, m, k * P:(k + 1) * P], ident[:, :])
                    mm.then_inc(turn_full[turn_by[n][0]], 1)
                elif kind in ("x1T", "x2T"):
                    p, n = step[1], turn_of[step]
                    pe.wait_ge(x1_ready if kind == "x1T" else x2_ready, p + 1)
                    bank = next_bank()
                    for k in range(KD):
                        mm = pe.transpose(bank[:, k * P:(k + 1) * P], X[:, p, k * P:(k + 1) * P], ident[:, :])
                    mm.then_inc(turn_full[turn_by[n][0]], 1)
                elif kind == "q":
                    m, n = step[1], work_of[step]
                    if m == 0:
                        wait_turned(pe, turn_of[("x1T", PAIRS - 2)], 1)
                        wait_turned(pe, turn_of[("x1T", PAIRS - 1)], 1)
                    bank = next_bank()
                    for k in range(KD):
                        mm = pe.matmul(bank[:, 0:B * T], wqT[:, k, m * P:(m + 1) * P],
                                       x1T[:, k, :, :].rearrange("p b t -> p (b t)"),
                                       start=(k == 0), stop=(k == KD - 1))
                    mm.then_inc(worked, 1)
                elif kind == "c_parts":
                    pe.wait_ge(cols_ready, 1)
                    pe.wait_ge(q_ready, KD)
                    bank = next_bank()
                    for k in range(KD):
                        mm = pe.matmul(bank[BL * k:BL * k + BL, :], bk_columns[:, k, :],
                                       qT[:, k, :, :].rearrange("p b t -> p (b t)"), start=True, stop=True)
                    mm.then_inc(worked, 1)
                elif kind == "c":
                    p, n = step[1], work_of[step]
                    pe.wait_ge(c_parts_ready, 1)
                    bank = next_bank()
                    pe.matmul(bank[:, 0:1], c_parts[:, 2 * TP * p:2 * TP * (p + 1)], mhalf[:, :],
                              start=True, stop=True).then_inc(worked, 1)
                elif kind == "g":
                    m, n = step[1], work_of[step]
                    if m == 0:
                        pe.wait_ge(wk_low_ready, 1)
                    bank = next_bank()
                    for k in range(KD):
                        if m == 0:
                            pe.wait_ge(q_low_ready, k + 1)
                        at = slice(m * P, (m + 1) * P)
                        pe.matmul(bank[:, 0:B * T], wk_high[:, k, at], q_high[:, k], start=(k == 0), stop=False)
                        pe.matmul(bank[:, 0:B * T], wk_high[:, k, at], q_low[:, k], start=False, stop=False)
                        mm = pe.matmul(bank[:, 0:B * T], wk_low[:, k, at], q_high[:, k],
                                       start=False, stop=(k == KD - 1))
                    mm.then_inc(worked, 1)
                elif kind == "ctxT":
                    _, j, g, h = step
                    b = 2 * j + h
                    wait_ctx(pe, b, g)
                    for kd in range(KD):
                        n = turn_of[step] + kd
                        bank = next_bank()
                        for k in range(KG):
                            mm = pe.transpose(bank[:, k * Q:(k + 1) * Q],
                                              ctx_sb[0:Q, b % SLOTS, KG * g + k, kd * P:(kd + 1) * P],
                                              ident[0:Q, 0:Q])
                        mm.then_inc(turn_full[turn_by[n][0]], 1)
                elif kind == "scores":
                    _, j, g = step
                    if j == 0 and g == 0:
                        pe.wait_ge(g_ready, 2 * KD)
                        pe.wait_ge(g_dve_ready, 2 * KD)
                    if j >= 1:
                        pe.wait_ge(exp_ready, GROUPS * (j - 1) + g + 1)
                        if g == GROUPS - 1:
                            pe.wait_ge(att_added, j)
                    by_blocks = ("cross", j, g, 0) in CROSS
                    if not by_blocks:
                        wait_turned(pe, turn_of[("ctxT", j, g, 0)], KD)
                        wait_turned(pe, turn_of[("ctxT", j, g, 1)], KD)
                        pe.wait_ge(g_tiles_ready, KD)
                    for kd in range(KD):
                        for h in range(2):
                            if by_blocks:
                                pe.wait_ge(crossed, KD * CROSS.index(("cross", j, g, h)) + kd + 1)
                            g_piece = gT[:, kd, 2 * j + h, :] if by_blocks else gT_tiles[:, kd, 2 * j - 2 + h, :]
                            mm = pe.matmul(psS[h * TP:(h + 1) * TP, g, 0:GC], g_piece,
                                           ctxT[:, (GROUPS * j + g) % 2, h, kd, 0:GC],
                                           start=(kd == 0), stop=(kd == KD - 1))
                    mm.then_inc(scored, 1)
                elif kind == "pT":
                    j = step[1]
                    for g in range(GROUPS):
                        n = turn_of[step] + g
                        pe.wait_ge(exp_ready, GROUPS * j + g + 1)
                        bank = next_bank()
                        for k in range(KG):
                            mm = pe.transpose(bank[0:Q, k * P:(k + 1) * P], prob[:, KG * g + k, :], ident[:, :])
                        mm.then_inc(turn_full[turn_by[n][0]], 1)
                elif kind == "attend":
                    j = step[1]
                    for g in range(GROUPS):
                        wait_turned(pe, turn_of[("pT", j)] + g)
                        for b in (2 * j, 2 * j + 1):
                            wait_ctx(pe, b, g)
                        for k in range(KG * g, KG * g + KG):
                            for h in range(2):
                                mm = pe.matmul(psA[h * TP:(h + 1) * TP, :], probT[0:Q, k, h * TP:(h + 1) * TP],
                                               ctx_sb[0:Q, (2 * j + h) % SLOTS, k, :],
                                               start=(k == 0), stop=(k == KT - 1))
                        mm.then_inc(attended, 1)
                elif kind == "proj":
                    group = step[1]
                    if group[0] == 0:
                        pe.wait_ge(u1_in, 16)
                    bank = next_bank()
                    for part in [q for q in (group[:-1], group[-1:]) if q]:
                        for p in part:
                            wait_turned(pe, turn_of[("x2T", p)])
                        to, at, N = 2 * T * (part[0] - group[0]), 2 * T * part[0], columns(part)
                        for k in range(KD):
                            mm = pe.matmul(bank[:, to:to + N], u1[:, k, :], x2T[:, k, at:at + N],
                                           start=(k == 0), stop=(k == KD - 1))
                    mm.then_inc(worked, 1)
                elif kind == "ffn":
                    _, group, c = step
                    n, N, f = work_of[step], columns(group), piece(c)
                    if c == 0:
                        pe.wait_ge(v1_in, 16)
                        pe.wait_ge(pr_ready, FFN_COUNT[group] + 1)
                    bank = next_bank()
                    if group == FFN_FIRST:
                        if c == 0:
                            pe.wait_ge(pr_low_ready, 1)
                        pe.wait_ge(v1_low_ready, 1 if c < SPLIT else 2)
                        for h in range(2):
                            at = h * INTER + c * P
                            high = v1_high[:, at:at + f]
                            pe.matmul(bank[0:f, 0:N], high, pr_high, start=True, stop=False)
                            pe.matmul(bank[0:f, 0:N], high, pr_low, start=False, stop=False)
                            pe.matmul(bank[0:f, 0:N], v1_low[:, at:at + f], pr_high,
                                      start=False, stop=True).then_inc(worked, 1)
                            if h == 0:
                                bank = next_bank()
                    else:
                        pe.matmul(bank[0:f, 0:N], v1[:, c * P:c * P + f], prT[:, 0:N], start=True, stop=True)
                        pe.matmul(bank[0:f, HALF:HALF + N], v1[:, INTER + c * P:INTER + c * P + f], prT[:, 0:N],
                                  start=True, stop=True).then_inc(worked, 1)
                    if c >= LAG:
                        inner_sum(group, c - LAG)
                elif kind == "ffn_sum":
                    for c in range(FC - LAG, FC):
                        inner_sum(step[1], c)
                elif kind == "ffn_out":
                    p = step[1]
                    pe.wait_ge(v2_in, 16)
                    pe.wait_ge(z_ready, 1 if p in FFN_FIRST else 2)
                    bank = next_bank()
                    pe.matmul(bank[:, :], zT[:, p].rearrange("p b t -> p (b t)"), v2[:, :],
                              start=True, stop=True).then_inc(worked, 1)

        @block.vector
        def _(ve):
            chained = [0]

            def link(ins):
                chained[0] += 1
                ins.then_inc(dve_chain, 1)
                ve.wait_ge(dve_chain, chained[0])

            nc.vector.memset(zeros, 0.0).then_inc(zeros_ready, 1)
            nc.vector.memset(probT[:, 2 * H, :], 0.0)
            nc.vector.memset(rows[:, :], 0.0).then_inc(rows_zero, 1)
            ve.wait_ge(bv_in, 48)
            link(nc.vector.tensor_scalar(sign, bv, 0.0, 2.0, ALU.is_ge, ALU.mult))
            link(nc.vector.scalar_tensor_tensor(out=bound, in0=sign, scalar=-1.0, in1=bv, op0=ALU.add, op1=ALU.mult,
                                                accum_out=asum[:, :]))
            link(nc.vector.tensor_scalar(bound, sign, -1.0, asum[:, :], ALU.add, ALU.mult))
            link(nc.vector.scalar_tensor_tensor(out=bound, in0=bound, scalar=1.0 / HD, in1=bv,
                                                op0=ALU.mult, op1=ALU.subtract))
            nc.vector.tensor_tensor(bv, bound, bv, ALU.add).then_inc(bound_ready, 1)

            def empty_turns(step, count):
                for i in range(count):
                    n = turn_of[step] + i
                    if turn_by[n][0] == 1:
                        wait_turn_full(ve, n)
                        o, src = turned_into(step, i)
                        nc.vector.tensor_copy(o, src).then_inc(turned[1], 1)

            def moments(layer, p):
                link(nc.vector.bn_stats(stats[:, layer, p, :], X[:, p, :]))
                nc.vector.bn_aggr(mv[:, layer, p, :], stats[:, layer, p, :]).then_inc(var_ready, 1)

            def normalize(layer, p):
                ve.wait_ge(rstd_ready, NORMS.index((layer, p)) + 1)
                return nc.vector.tensor_scalar(X[:, p, :], X[:, p, :], mv[:, layer, p, 0:1], rstd[:, layer, p:p + 1],
                                               ALU.subtract, ALU.mult)

            for step in STEPS:
                kind = step[0]
                if kind == "bind":
                    ve.wait_ge(worked, work_of[step] + 1)
                    link(nc.vector.tensor_copy(bcols[:, :], work(work_of[step])[:, 0:3 * H]))
                    nc.vector.tensor_tensor(qkc[:, :], bcols[:, H:2 * H], bcols[:, 2 * H:3 * H],
                                            ALU.mult).then_inc(qkc_ready, 1)
                elif kind == "columns":
                    ve.wait_ge(worked, work_of[step] + 1)
                    link(nc.vector.tensor_copy(cols[:, :], work(work_of[step])[:, 0:NROW]))
                    nc.vector.tensor_copy(bk_columns[:, :, 0:1],
                                          cols[:, KD:2 * KD].rearrange("p (k a) -> p k a", a=1))
                    nc.vector.tensor_scalar(hcols[:, :], cols[:, 2 * KD:NROW], 0.5, None,
                                            ALU.mult).then_inc(cols_ready, 1)
                elif kind in ("wqT", "x1T"):
                    empty_turns(step, 1)
                elif kind == "x2T":
                    if step[1] == 0:
                        ve.wait_ge(worked, work_of[("c_parts",)] + 1)
                    empty_turns(step, 1)
                elif kind == "ctxT":
                    _, j, g, h = step
                    n = GROUPS * j + g
                    if n >= 2 and h == 0:
                        ve.wait_ge(scored, n - 1)
                    empty_turns(step, KD)
                elif kind == "cross":
                    _, j, g, h = step
                    if h == 0 and GROUPS * j + g >= 2:
                        ve.wait_ge(scored, GROUPS * j + g - 1)
                    buffer, loaded, loads = block_buffer(step)
                    ve.wait_ge(loaded, 16 * loads)
                    by_piece = buffer.rearrange("p n (k r) -> p k n r", k=KD)
                    for kd in range(KD):
                        nc.vector.transpose(ctxT[:, (GROUPS * j + g) % 2, h, kd, :].rearrange("p (n r) -> p n r", r=BL),
                                            by_piece[:, kd]).then_inc(crossed, 1)
                elif kind == "pT":
                    if step[1] >= 1:
                        ve.wait_ge(attended, GROUPS * step[1])
                    empty_turns(step, GROUPS)
                elif kind == "self_scores":
                    p, n = step[1], work_of[step]
                    if p == 0:
                        ve.wait_ge(consts, 2)
                    ve.wait_ge(tanh_ready, p + 1)
                    nc.vector.scalar_tensor_tensor(
                        out=selfp[:, p % 2], in0=selfp[:, p % 2], scalar=1.0,
                        in1=mask[:, :].rearrange("p (a t) -> p a t", a=1).to_broadcast([P, H, P]),
                        op0=ALU.add, op1=ALU.mult).then_inc(selfp_ready, 1)
                elif kind == "self_out":
                    p, n = step[1], work_of[step]
                    ve.wait_ge(worked, n + 1)
                    ve.wait_ge(val_ready, p + 1)
                    nc.vector.tensor_tensor(X[:, p, :], work(n), X[:, p, :], ALU.add).then_inc(self_added, 1)
                    ve.wait_ge(self_added, p + 1)
                    moments(0, p)
                elif kind == "q":
                    m = step[1]
                    ve.wait_ge(q_high_ready, m + 1)
                    nc.vector.tensor_tensor(q_low[:, m].rearrange("p (b t) -> p b t", b=B), qT[:, m, :, 0:T],
                                            q_high[:, m].bitcast(F32).rearrange("p (b t) -> p b t", b=B),
                                            ALU.subtract).then_inc(q_low_ready, 1)
                elif kind == "wk_split":
                    ve.wait_ge(wk_high_ready, 1)
                    nc.vector.tensor_tensor(wk_low, wkv, wk_high.bitcast(F32), ALU.subtract).then_inc(wk_low_ready, 1)
                elif kind == "g":
                    m, n = step[1], work_of[step]
                    ve.wait_ge(worked, n + 1)
                    if m == 0:
                        ve.wait_ge(consts, 3)
                    for k in (2, 3):
                        nc.vector.tensor_copy(gT[BL * m:BL * m + BL, k, :, 0:T],
                                              work(n)[BL * k:BL * k + BL, 0:B * T].rearrange("p (b t) -> p b t", b=B))\
                          .then_inc(g_dve_ready, 1)
                    ve.wait_ge(g_ready, 2 * (m + 1))
                    nc.vector.tensor_copy(gT_tiles[:, m, :, 0:T],
                                          work(n)[:, 2 * T:B * T].rearrange("p (b t) -> p b t", b=B - 2))\
                      .then_inc(g_tiles_ready, 1)
                elif kind == "c":
                    p, n = step[1], work_of[step]
                    ve.wait_ge(worked, n + 1)
                    nc.vector.tensor_scalar(c_sb[:, p:p + 1], work(n)[:, 0:1], -2.0, None,
                                            ALU.mult).then_inc(c_ready, 1)
                    if p == PAIRS - 1:
                        ve.wait_ge(c_ready, PAIRS)
                elif kind == "scores":
                    _, j, g = step
                    ve.wait_ge(scored, GROUPS * j + g + 1)
                    last = nc.vector.reduce_max(top[:, g:g + 1], psS[:, g, 0:GC], AX.X)
                    if g == GROUPS - 1:
                        link(last)
                elif kind == "bias":
                    j = step[1]
                    link(nc.vector.reduce_max(topc[:, :], top[:, :], AX.X))
                    link(nc.vector.tensor_tensor(topc[:, :], topc[:, :], c_sb[:, j:j + 1], ALU.add))
                    nc.vector.tensor_scalar(bias[:, :], topc[:, :], c_sb[:, j:j + 1], -X_SCALE,
                                            ALU.subtract, ALU.mult).then_inc(bias_ready, 1)
                elif kind == "attend":
                    j = step[1]
                    ve.wait_ge(exp_ready, GROUPS * (j + 1))
                    link(nc.vector.reduce_sum(dsum[:, :], den[:, :], AX.X))
                    link(nc.vector.reciprocal(rden[:, :], dsum[:, :]))
                    ve.wait_ge(attended, GROUPS * (j + 1))
                    nc.vector.scalar_tensor_tensor(out=X[:, j, :], in0=psA[:, :], scalar=rden[:, :],
                                                   in1=X[:, j, :], op0=ALU.mult, op1=ALU.add).then_inc(att_added, 1)
                    ve.wait_ge(att_added, j + 1)
                    moments(1, j)
                elif kind == "proj" and step[1] == FFN_FIRST:
                    ve.wait_ge(pr_ready, 1)
                    nc.vector.tensor_tensor(pr_low, work(work_of[step])[:, 0:NMAX], pr_high.bitcast(F32),
                                            ALU.subtract).then_inc(pr_low_ready, 1)
                elif kind == "split":
                    ve.wait_ge(v1_high_ready, step[1] + 1)
                    nc.vector.tensor_tensor(split_columns(step[1], v1_low), split_columns(step[1], v1),
                                            split_columns(step[1], v1_high.bitcast(F32)),
                                            ALU.subtract).then_inc(v1_low_ready, 1)
                elif kind == "norm2":
                    normalize(1, step[1]).then_inc(x2_ready, 1)
                elif kind == "ffn":
                    _, group, c = step
                    n, N, f = work_of[step], columns(group), piece(c)
                    i = FFN_COUNT[group] * FC + c
                    ve.wait_ge(gate_ready, i + 1)
                    link(nc.vector.scalar_tensor_tensor(out=tanh[0:f, i % GB, 0:N], in0=tanh[0:f, i % GB, 0:N],
                                                        scalar=1.0, in1=gate[0:f, i % GB, 0:N],
                                                        op0=ALU.add, op1=ALU.mult))
                    ve.wait_ge(worked, n + banks_of(group))
                    if c == 0 and FFN_COUNT[group] >= 1:
                        ve.wait_ge(summed, FFN_COUNT[group])
                    nc.vector.scalar_tensor_tensor(out=act[0:f, c, 0:N], in0=gated(group, n)[0:f, 0:N],
                                                   scalar=cols[0:f, 2 * KD + FC + c:2 * KD + FC + c + 1],
                                                   in1=tanh[0:f, i % GB, 0:N],
                                                   op0=ALU.add, op1=ALU.mult).then_inc(act_ready, 1)
                elif kind == "ffn_out":
                    p, n = step[1], work_of[step]
                    ve.wait_ge(worked, n + 1)
                    ve.wait_ge(x2b_ready, p + 1)
                    nc.vector.tensor_tensor(X[:, p, :], work(n), X[:, p, :], ALU.add).then_inc(y_added, 1)
                    ve.wait_ge(y_added, OUTS.index(p) + 1)
                    moments(2, p)
                elif kind == "norm3" and step[1] == STORES[-1]:
                    ve.wait_ge(y_ready, PAIRS - 1)
                    normalize(2, step[1]).then_inc(y_ready, 1)


_INS = ['x', 'ctx_4096', 'L0_attn_bv_q', 'L0_attn_bv_k', 'L0_attn_bv_v', 'L0_xattn_Wq', 'L0_xattn_bq', 'L0_xattn_Wk',
        'L0_xattn_bk', 'L0_ffn_U1', 'L0_ffn_V1', 'L0_ffn_U2', 'L0_ffn_V2', 'L0_ffn_b1', 'L0_ffn_b2']


def kernel(**inputs):
    import numpy as _np
    import concourse.bacc as _bacc
    from concourse import mybir as _mybir
    from concourse.bass_utils import run_bass_kernel_spmd as _run

    nc = _bacc.Bacc("TRN2", target_bir_lowering=False, num_devices=1)
    arrays, args = {}, []
    for name in _INS:
        a = _np.ascontiguousarray(inputs[name])
        arrays[f"in_{name}_dram"] = a
        args.append(nc.dram_tensor(f"in_{name}_dram", a.shape, _mybir.dt.from_np(a.dtype), kind="ExternalInput").ap())
    shape = inputs['x'].shape
    out = nc.dram_tensor("out_dram", shape, _mybir.dt.from_np(_np.dtype('float32')), kind="ExternalOutput").ap()
    decoder_layer(nc, *args, out)
    r = _run(nc, [arrays], core_ids=[0])
    return r.results[0]["out_dram"]
```
